# Optimizing a Trainium2 kernel written in Bass

```python
import numpy as np
import jax
import jax.numpy as jnp

def _softmax(x, axis=-1):
    return jax.nn.softmax(x, axis=axis)

def _gelu(x):
    return jax.nn.gelu(x, approximate=True)

def _silu(x):
    return jax.nn.silu(x)

def _sigmoid(x):
    return jax.nn.sigmoid(x)

def _layernorm(x, axis=-1, eps=1e-05):
    m = jnp.mean(x, axis=axis, keepdims=True)
    v = jnp.var(x, axis=axis, keepdims=True)
    return (x - m) / jnp.sqrt(v + eps)

def _scatter_add(tgt, idx, src, axis=0):
    return tgt.at[idx].add(src)

def _segment_sum(src, seg, n):
    return jax.ops.segment_sum(src, seg, n)
kernel_name = 'mk_adj_preln_d2_adj_r2_772926'

def setup_inputs(seed: int=0):
    np.random.seed(seed)
    _w = jnp.asarray

    def _rec_inputs():
        import jax
        import jax.numpy as jnp
        _gk = jax.random.key(seed)
        x = -0.0005207 + 1.001 * jax.random.normal(jax.random.fold_in(_gk, 1), (8192, 128), jnp.float32)
        _a = jax.random.bernoulli(jax.random.fold_in(_gk, 2), 0.000976562, (8192, 8192))
        _a = jnp.logical_or(_a, jnp.swapaxes(_a, -1, -2))
        _a = jnp.logical_or(_a, jnp.eye(8192, dtype=bool))
        _af = _a.astype(jnp.float32)
        adj = _af
        return (x, adj)
    x, adj = _rec_inputs()

    def _L0_gnn_setup():
        import jax, jax.numpy as jnp
        import numpy as np
        N = 4096
        IN_F = 128
        OUT_F = 128
        ATTN_DIM = 2
        NEG_INF = -1e+18
        key = jax.random.key(seed)
        k1, k2, k3, k4, k5 = jax.random.split(key, 5)
        node_feats = jax.random.normal(k1, (N, IN_F), dtype=jnp.float32)
        Ahat = (jax.random.uniform(k2, (N, N)) < 0.01).astype(jnp.float32)
        Ahat = Ahat.at[jnp.arange(N), jnp.arange(N)].set(1.0)
        bound_w = 1.0 / np.sqrt(IN_F)
        bound_wa = 1.0 / np.sqrt(OUT_F)
        bound_a = 1.0 / np.sqrt(2 * ATTN_DIM)
        w = jax.random.uniform(k3, (IN_F, OUT_F), minval=-bound_w, maxval=bound_w, dtype=jnp.float32)
        w_a = jax.random.uniform(k4, (OUT_F, ATTN_DIM), minval=-bound_wa, maxval=bound_wa, dtype=jnp.float32)
        a = jax.random.uniform(k5, (2 * ATTN_DIM, 1), minval=-bound_a, maxval=bound_a, dtype=jnp.float32)
        return {'node_feats': node_feats, 'Ahat': Ahat, 'w': w, 'w_a': w_a, 'a': a}
    _L0_gnn_all = _L0_gnn_setup()
    _L0_gnn_in = {k: v for k, v in _L0_gnn_all.items() if k in ('w', 'w_a', 'a')}
    del _L0_gnn_all

    def _L1_gnn_setup():
        import jax, jax.numpy as jnp
        import numpy as np
        N, F_IN, F_OUT = (4096, 128, 128)
        key = jax.random.key(seed)
        k1, k2, k3, k4 = jax.random.split(key, 4)
        X = jax.random.normal(k1, (N, F_IN), dtype=jnp.float32)
        A = jax.random.uniform(k2, (N, N), dtype=jnp.float32)
        W = jax.random.normal(k3, (F_OUT, F_IN), dtype=jnp.float32) * (1.0 / np.sqrt(F_IN))
        b = jax.random.normal(k4, (F_OUT,), dtype=jnp.float32) * 0.01
        return {'X': X, 'A': A, 'W': W, 'b': b}
    _L1_gnn_all = _L1_gnn_setup()
    _L1_gnn_in = {k: v for k, v in _L1_gnn_all.items() if k in ('W', 'b')}
    del _L1_gnn_all
    return {'x': x, 'adj': adj, 'L0_gnn_w': _L0_gnn_in['w'], 'L0_gnn_w_a': _L0_gnn_in['w_a'], 'L0_gnn_a': _L0_gnn_in['a'], 'L1_gnn_W': _L1_gnn_in['W'], 'L1_gnn_b': _L1_gnn_in['b']}

def reference(x, adj, L0_gnn_w, L0_gnn_w_a, L0_gnn_a, L1_gnn_W, L1_gnn_b):
    import jax
    import jax.numpy as jnp

    def _L0_gnn_ref(node_feats, Ahat, w, w_a, a):
        import jax, jax.numpy as jnp
        import numpy as np
        N = 4096
        IN_F = 128
        OUT_F = 128
        ATTN_DIM = 2
        NEG_INF = -1e+18
        h_prime = node_feats @ w
        h_reduced = h_prime @ w_a
        f_src = (h_reduced @ a[:ATTN_DIM]).squeeze(-1)
        f_dst = (h_reduced @ a[ATTN_DIM:]).squeeze(-1)
        e = f_src[:, None] + f_dst[None, :]
        masked_e = jnp.where(Ahat > 0, e, NEG_INF)
        attn_scores = jax.nn.softmax(masked_e, axis=-1)
        out = attn_scores @ h_prime
        return jax.nn.relu(out)

    def _L1_gnn_ref(X, A, W, b):
        import jax, jax.numpy as jnp
        import numpy as np
        N, F_IN, F_OUT = (4096, 128, 128)
        A_hat = A + jnp.eye(A.shape[0], dtype=A.dtype)
        deg = jnp.sum(A_hat, axis=1)
        d = jnp.where(deg > 0, jax.lax.rsqrt(deg), 0.0)
        A_norm = d[:, None] * A_hat * d[None, :]
        out = A_norm @ X
        out = out @ W.T + b
        return out
    h = jnp.maximum(_layernorm(x, axis=-1), 0.0)
    x = x + _L0_gnn_ref(h, adj, L0_gnn_w, L0_gnn_w_a, L0_gnn_a)
    h = jnp.maximum(_layernorm(x, axis=-1), 0.0)
    x = x + _L1_gnn_ref(h, adj, L1_gnn_W, L1_gnn_b)
    return x

_drawn_inputs = setup_inputs


def setup_inputs(seed=0):
    import zlib

    import numpy as np

    out = dict(_drawn_inputs(seed))
    spreads = {}
    factors = {'L0_gnn_w_a': 8.0, 'L0_gnn_a': 8.0, 'L1_gnn_b': 6.058}
    for name, (base, spread) in spreads.items():
        noise = np.random.default_rng([zlib.crc32(name.encode()), seed]).standard_normal(out[name].shape)
        drawn = base * np.exp(spread * noise) if base else spread * noise
        out[name] = jnp.asarray(drawn.astype(out[name].dtype))
    for name, factor in factors.items():
        out[name] = (out[name] * factor).astype(out[name].dtype)
    return out
```

```python
from contextlib import ExitStack
import math

import numpy as np
import concourse.bass as bass
from concourse import mybir

F32, F16, BF16 = mybir.dt.float32, mybir.dt.float16, mybir.dt.bfloat16
U8, U16, U32, I32 = mybir.dt.uint8, mybir.dt.uint16, mybir.dt.uint32, mybir.dt.int32
ALU = mybir.AluOpType
ACT = mybir.ActivationFunctionType
AX = mybir.AxisListType

P = 128
N = 8192
D = 128
T = N // P
BL = 4
SB = T // BL
IW = BL * P
CT = 4
CH = T // CT
OCT = 8
NSTAGE = 4
NMASK = 4
EPS = 1e-5

LOG2E = float(np.float32(1.0 / math.log(2.0)))
LN2_HI = float(np.float32(0.693359375))
LN2_LO = float(np.float32(math.log(2.0) - 0.693359375))
ROUND = float(3 << 22)
TOP = 60
BUCKETS = 4
LOW = TOP - 30 * BUCKETS + 1
M_SCALE = 1024.0
NV0 = 2 * D + 2 + BUCKETS
BOUND = 2.0 ** 14 / (math.sqrt(D) * 1.42)

GROUPS = [(0, 1, 0), (1, 1, 0), (2, 1, 1), (3, 1, 1)] + [(2 * p, 2, p) for p in range(2, SB // 2)]
OCTETS = [s // 2 for s in range(SB)]
EARLY = sum(OCTETS)
FIRST_L1 = 2
ROW_STEPS = 5


def octets_before(s, first, octets):
    return sum(OCTETS[:first]) + (s - first) * octets


def octets_through_late(s):
    return EARLY + sum(SB // 2 - o for o in OCTETS[:s + 1])


def build(nc, ins, outs):
    adj, x_in, w_in, wT_in, waT_in, a_in, WT_in, b_in = ins
    out = outs
    y_dram = nc.dram_tensor("y_scratch", (P, SB, BL, D), F32, kind="Internal").ap()
    ctx = ExitStack()

    def sb(name, shape, dt):
        return ctx.enter_context(nc.sbuf_tensor(name, shape, dt))

    def sem(name):
        return ctx.enter_context(nc.semaphore(name))

    bits = sb("bits", [P, SB, OCT * IW], U8)
    V0 = sb("V0", [P, T, NV0], F16)
    V1 = sb("V1", [P, T, 2 * D], F16)
    stage = sb("stage", [P, NSTAGE, CT * IW], F32)
    mask = sb("mask", [P, NMASK, CT * IW], BF16)
    byte = sb("byte", [P, 2, CT * IW], U8)
    unp = sb("unp", [P, 2, 2, OCT * IW // 2], F16)
    ev = sb("ev", [P, BL, NV0], F32)
    num = sb("num", [P, BL, D], F32)
    xb = sb("xb", [P, BL, D], F32)
    ident = sb("ident", [P, P], F32)
    ident2 = sb("ident2", [P, P], F16)
    WT = sb("WT", [P, D], F32)
    bias = sb("bias", [P, D], F32)
    meanh = sb("meanh", [P, D], F32)
    scale2 = sb("scale2", [P, T], F32)
    dall = sb("dall", [P, T], F32)
    sig = sb("sig", [P, 8], F32)
    cw = sb("cw", [P, BUCKETS], F32)
    den = sb("den", [P, BL], F32)
    cprod = sb("cprod", [P, BL, BUCKETS], F32)
    zero_row = sb("zero_row", [P, BL], F32)
    cnt = sb("cnt", [P, BL], F32)
    rden = sb("rden", [P, BL], F32)
    bst = sb("bst", [P, BL, 6], F32)
    bmv = sb("bmv", [P, BL, 2], F32)
    sq = sb("sq", [P, 2 * BL], F32)
    rs = sb("rs", [P, 2 * BL], F32)
    nbias = sb("nbias", [P, BL], F32)
    dsig = sb("dsig", [P, BL], F32)
    dback = sb("dback", [P, BL], F32)
    zcol = sb("zcol", [P, 1], F32)

    low_half = bits[:, 0:SB // 2, :].rearrange("p s n -> p (s n)").bitcast(F32)
    high_half = bits[:, SB // 2:SB, :].rearrange("p s n -> p (s n)").bitcast(F32)
    X = low_half.rearrange("p (t f) -> p t f", f=D)
    H = high_half.rearrange("p (t f) -> p t f", f=D)
    v1f = V1[:, :, :].rearrange("p t f -> p (t f)").bitcast(F32)
    hT = [v1f[:, 512 * k:512 * k + 512] for k in range(2)]
    at = [1024]

    def small(n):
        a = at[0]
        at[0] += n
        return v1f[:, a:a + n]

    ones = small(P)
    wG = small(D + 1)
    wTt = small(D)
    waT = small(D)
    a2 = small(1)
    wa2 = small(1)
    wsq = small(2 * D)
    cmax = small(2)
    st = small(T * 6).rearrange("p (t k) -> p t k", k=6)
    mv = small(T * 2).rearrange("p (t k) -> p t k", k=2)
    sd = small(T)
    rstd = small(T)
    epsc = small(1)
    hsum = small(16)
    hsum1 = small(1)
    hb = small(P)
    f = small(T)
    kf = small(T)
    r1 = small(T)
    m = small(T)
    mS = small(T)
    kmax = small(1)
    kall = small(1)
    ke = small(T)
    sbit = small(T).bitcast(I32)
    w15 = [small(T) for _ in range(BUCKETS)]
    q1 = [small(T) for _ in range(BUCKETS)]
    q2 = [small(T) for _ in range(BUCKETS)]

    ps0 = ctx.enter_context(nc.psum_tensor("ps0", [P, BL, 512], F32))
    ps1 = ctx.enter_context(nc.psum_tensor("ps1", [P, 2, 512], F32))
    psT = ctx.enter_context(nc.psum_tensor("psT", [P, 512], F32))
    psH = ctx.enter_context(nc.psum_tensor("psH", [P, 512], F32))
    setT = [psT, psH]
    setH = [ps0[:, 0:2, :], ps0[:, 2:4, :]]

    weights_in = sem("weights_in")
    x_part = [sem(f"x_part{q}") for q in range(4)]
    pool_consts = sem("pool_consts")
    vec_consts = sem("vec_consts")
    std_done = sem("std_done")
    normed = sem("normed")
    g_mm = sem("g_mm")
    g_cp = sem("g_cp")
    tr_done = sem("tr_done")
    hT_done = sem("hT_done")
    hp_mm = sem("hp_mm")
    hp_cp = sem("hp_cp")
    norm_sqrt = sem("norm_sqrt")
    mean_mm = sem("mean_mm")
    mean_cp = sem("mean_cp")
    hb_done = sem("hb_done")
    var_done = sem("var_done")
    norms_done = sem("norms_done")
    wsq_done = sem("wsq_done")
    frac_done = sem("frac_done")
    kmax_done = sem("kmax_done")
    v0_cols = sem("v0_cols")
    vec_step = sem("vec_step")
    exp_done = sem("exp_done")
    kall_done = sem("kall_done")
    v0_f32 = sem("v0_f32")
    v0_hi = sem("v0_hi")
    v0_lo = sem("v0_lo")
    adj_landed = [sem(f"adj_landed{k}") for k in range(NSTAGE)]
    mask_ready = sem("mask_ready")
    byte_ready = sem("byte_ready")
    packed = sem("packed")
    l0_done = sem("l0_done")
    unpacked = sem("unpacked")
    l1_octet = sem("l1_octet")
    x_loaded = sem("x_loaded")
    ev_ready = sem("ev_ready")
    row_step = sem("row_step")
    z_ready = sem("z_ready")
    xz_ready = sem("xz_ready")
    x1_ready = sem("x1_ready")
    sq_ready = sem("sq_ready")
    sqrt_done = sem("sqrt_done")
    rs_ready = sem("rs_ready")
    h_ready = sem("h_ready")
    rowT_done = sem("rowT_done")
    rowT_copied = sem("rowT_copied")
    rowW_done = sem("rowW_done")
    v_ready = sem("v_ready")
    v1_hi = sem("v1_hi")
    v1_ready = sem("v1_ready")
    l1_low = sem("l1_low")
    l1_scaled = sem("l1_scaled")
    biased = sem("biased")
    zrow_done = sem("zrow_done")
    rstat_done = sem("rstat_done")
    rs_recip = sem("rs_recip")
    dall_done = sem("dall_done")
    l1_sum = sem("l1_sum")
    y_ready = sem("y_ready")
    y_stored = sem("y_stored")
    tail_x = [sem(f"tail_x{k}") for k in range(2)]
    tail_low = sem("tail_low")
    tail_sum = sem("tail_sum")
    tail_scaled = sem("tail_scaled")
    tail_out = sem("tail_out")
    out_stored = [sem(f"out_stored{k}") for k in range(2)]

    def wait(eng, s, value):
        if not isinstance(value, int) or value > 0:
            eng.wait_ge(s, value)

    def superblocks(eng, body):
        for first, count, octets in GROUPS:
            if count == 1:
                body(first, first, octets)
            else:
                with eng.Fori(first, first + count) as s:
                    body(s, first, octets)

    def wide(v):
        return v.unsqueeze(2).broadcast_to([P, v.shape[1], D])

    def per_block(v):
        return v.unsqueeze(1).broadcast_to([P, BL, D])

    def tail_ps(s):
        return ps0[:, 2 * (s % 2):2 * (s % 2) + 2, :]

    def tail_part(s):
        return ev[:, :, D * (s % 2):D * (s % 2) + D]

    def copy_products(act, g):
        act.wait_ge(hp_mm, g + 1)
        src = setH[g % 2][:, :, 0:2 * (D + 1)].rearrange("p a (b f) -> p a b f", b=2)
        nc.scalar.activation(H[:, 4 * g:4 * g + 4, :].rearrange("p (a b) f -> p a b f", b=2), src[:, :, :, 0:D], ACT.Copy)
        nc.scalar.activation(f[:, 4 * g:4 * g + 4].rearrange("p (a b) -> p a b", b=2), src[:, :, :, D],
                             ACT.Copy).then_inc(hp_cp, 1)

    V1s = V1[:, :, :].rearrange("p (s b) f -> p s b f", b=BL)
    dalls = dall[:, :].rearrange("p (s b) -> p s b", b=BL)

    block = ctx.enter_context(nc.Block())

    @block.sync
    def _(sp):
        for q in range(4):
            sp.dma_start(X[:, 16 * q:16 * q + 16, :],
                         x_in[:, 4 * q:4 * q + 4].rearrange("p s b f -> p (s b) f")).then_inc(x_part[q], 16)

        def body(s, first, octets):
            for c in range(CH):
                n = CH * s + c
                wait(sp, mask_ready, n - NSTAGE + 1)
                wait(sp, byte_ready, n - NSTAGE + 1)
                sp.dma_start(stage[:, c % NSTAGE, :], adj[s, c]).then_inc(adj_landed[c % NSTAGE], 16)
                if c == 13:
                    wait(sp, y_stored, 16 * s)
                    sp.dma_start(xb[:, :, :], x_in[:, s]).then_inc(x_loaded, 16)

        superblocks(sp, body)

        for s in range(SB + 2):
            if s < SB:
                if s == 0:
                    sp.wait_ge(y_stored, 16 * SB)
                    sp.wait_ge(v1_ready, SB)
                if s >= 2:
                    sp.wait_ge(out_stored[s % 2], 16 * (s // 2))
                sp.dma_start([xb, num][s % 2][:, :, :], y_dram[:, s]).then_inc(tail_x[s % 2], 16)
            if 1 <= s <= SB:
                sp.wait_ge(tail_out, s)
                sp.dma_start(out[:, s - 1], [xb, num][(s - 1) % 2][:, :, :]).then_inc(out_stored[(s - 1) % 2], 16)
        for k in range(2):
            sp.wait_ge(out_stored[k], 16 * SB // 2)

    @block.gpsimd
    def _(pool):
        nc.gpsimd.memset(ident[:], 0.0).then_inc(pool_consts, 1)
        pool.wait_ge(pool_consts, 1)
        nc.gpsimd.affine_select(out=ident[:], in_=ident[:], compare_op=ALU.not_equal, fill=1.0, base=0,
                                pattern=[[-1, P]], channel_multiplier=1).then_inc(pool_consts, 1)
        for b in range(BUCKETS):
            nc.gpsimd.memset(cw[:, b:b + 1], 2.0 ** -(TOP - 14 - 30 * b)).then_inc(pool_consts, 1)
        pool.wait_ge(kmax_done, 1)
        nc.gpsimd.partition_all_reduce(kall, kmax, P, bass.bass_isa.ReduceOp.max).then_inc(kall_done, 1)

        for q in range(4):
            pool.wait_ge(v0_hi, q + 1)
            nc.gpsimd.tensor_tensor(V0[:, 16 * q:16 * q + 16, D:2 * D], H[:, 16 * q:16 * q + 16, :],
                                    V0[:, 16 * q:16 * q + 16, 0:D], ALU.subtract).then_inc(v0_lo, 1)

        def rows(e, early):
            pool.wait_ge(z_ready, e + 1)
            nc.gpsimd.tensor_tensor(ev[:, :, 0:D], wide(zero_row[:, :]), per_block(meanh[:, :]),
                                    ALU.mult).then_inc(zrow_done, 1)
            pool.wait_ge(x_loaded, 16 * (e + 1))
            pool.wait_ge(zrow_done, e + 1)
            nc.gpsimd.tensor_tensor(xb[:, :, :], xb[:, :, :], ev[:, :, 0:D], ALU.add).then_inc(xz_ready, 1)
            pool.wait_ge(h_ready, e + 1)
            nc.gpsimd.tensor_tensor(xb[:, :, :], xb[:, :, :], per_block(bias[:, :]),
                                    ALU.add).then_inc(y_ready if not early else biased, 1)
            if early:
                pool.wait_ge(l1_sum, e - FIRST_L1 + 1)
                nc.gpsimd.tensor_tensor(ev[:, :, D:2 * D], ev[:, :, D:2 * D], wide(dback[:, :]),
                                        ALU.mult).then_inc(l1_scaled, 1)
                pool.wait_ge(l1_scaled, e - FIRST_L1 + 1)
                pool.wait_ge(biased, e - FIRST_L1 + 1)
                nc.gpsimd.tensor_tensor(xb[:, :, :], xb[:, :, :], ev[:, :, D:2 * D], ALU.add).then_inc(y_ready, 1)
            pool.wait_ge(v1_hi, e + 1)
            nc.gpsimd.tensor_tensor(V1s[:, e, :, D:2 * D], num[:, :, :], V1s[:, e, :, 0:D],
                                    ALU.subtract).then_inc(v1_ready, 1)

        rows(0, False)
        rows(1, False)
        with pool.Fori(FIRST_L1, SB) as e:
            rows(e, True)

    @block.scalar
    def _(act):
        for k, (dst, src) in enumerate([(wG[:, 0:D], w_in), (wTt, wT_in), (waT[0:2, :], waT_in), (a2[0:2, :], a_in),
                                        (WT[:, :], WT_in), (bias[:, :], b_in)]):
            act.dma_start(dst, src).then_inc(weights_in, 16)
        act.wait_ge(vec_consts, 3)
        for q in range(4):
            act.wait_ge(var_done, q + 1)
            nc.scalar.activation(sd[:, 16 * q:16 * q + 16], mv[:, 16 * q:16 * q + 16, 1], ACT.Sqrt,
                                 bias=epsc).then_inc(std_done, 1)
        act.wait_ge(norms_done, 1)
        nc.scalar.activation(cmax, cmax, ACT.Sqrt).then_inc(norm_sqrt, 1)
        for g in range(16):
            act.wait_ge(tr_done, g + 1)
            if g >= 2:
                act.wait_ge(hp_mm, g - 1)
            nc.scalar.activation(hT[g % 2], setT[g % 2][:, :], ACT.Relu,
                                 accum_out=hsum[:, g:g + 1]).then_inc(hT_done, 1)
            if g:
                copy_products(act, g - 1)
        copy_products(act, 15)
        act.wait_ge(frac_done, 1)
        nc.scalar.activation(m, r1, ACT.Exp).then_inc(exp_done, 1)
        for q in range(4):
            act.wait_ge(v0_f32, q + 1)
            nc.scalar.activation(V0[:, 16 * q:16 * q + 16, 0:D], H[:, 16 * q:16 * q + 16, :],
                                 ACT.Copy).then_inc(v0_hi, 1)

        def rows(e, after):
            if after == 0:
                act.wait_ge(l0_done, CH * (e + 1))
                wait(act, rowW_done, e)
                wait(act, y_ready, e)
                nc.scalar.activation(ev[:, :, :], ps0[:, :, 0:NV0], ACT.Copy).then_inc(ev_ready, 1)
            if after == 2:
                act.wait_ge(sq_ready, e + 1)
                nc.scalar.activation(rs[:, :], sq[:, :], ACT.Sqrt).then_inc(sqrt_done, 1)
            if after == 3:
                act.wait_ge(rs_ready, e + 1)
                for b in range(BL):
                    last = nc.scalar.activation(num[:, b, :], xb[:, b, :], ACT.Relu, bias=nbias[:, b:b + 1],
                                                scale=rs[:, b:b + 1])
                last.then_inc(h_ready, 1)
            if after == 4 and not (isinstance(e, int) and e < FIRST_L1):
                act.wait_ge(l1_octet, octets_through[0])
                nc.scalar.activation(ev[:, :, D:2 * D].rearrange("p (a b) f -> p a b f", b=2),
                                     ps1[:, :, :].rearrange("p a (b f) -> p a b f", b=2)[:, :, :, D:2 * D],
                                     ACT.Copy).then_inc(l1_low, 1)
            if after == 6:
                act.wait_ge(rowT_done, e + 1)
                nc.scalar.activation(ev[:, :, 0:D], psT[:, :].rearrange("p (b f) -> p b f", b=BL),
                                     ACT.Copy).then_inc(rowT_copied, 1)
            if after == 8:
                act.wait_ge(y_ready, e + 1)
                act.dma_start(y_dram[:, e], xb[:, :, :]).then_inc(y_stored, 16)
            if after == 9:
                act.wait_ge(v_ready, e + 1)
                nc.scalar.activation(V1s[:, e, :, 0:D], num[:, :, :], ACT.Copy).then_inc(v1_hi, 1)

        octets_through = [0]

        def body(s, first, octets):
            octets_through[0] = octets_before(s, first, octets)
            for c in range(CH):
                n = CH * s + c
                act.wait_ge(adj_landed[c % NSTAGE], 4 * 16 * s + 16 * (c // NSTAGE + 1))
                if c < 2:
                    dst = bits[:, s, c * CT * IW:(c + 1) * CT * IW]
                else:
                    wait(act, packed, 14 * s + (c - 2) - 1)
                    dst = byte[:, c % 2, :]
                nc.scalar.activation(dst.rearrange("p (a l r) -> p a r l", l=P, r=2),
                                     stage[:, c % NSTAGE, :].rearrange("p (a r l) -> p a r l", l=P, r=2),
                                     ACT.Copy).then_inc(byte_ready, 1)
                if not (isinstance(s, int) and s == 0):
                    rows(s - 1, c)

        superblocks(act, body)
        octets_through[0] = EARLY
        for c in range(CH):
            rows(SB - 1, c)

        for s in range(SB):
            act.wait_ge(l1_octet, octets_through_late(s))
            if s >= 2:
                act.wait_ge(tail_out, s - 1)
            nc.scalar.activation(tail_part(s).rearrange("p (a b) f -> p a b f", b=2),
                                 tail_ps(s).rearrange("p a (b f) -> p a b f", b=2)[:, :, :, D:2 * D],
                                 ACT.Copy).then_inc(tail_low, 1)

    @block.tensor
    def _(pe):
        pe.wait_ge(weights_in, 96)
        nc.tensor.matmul(ps1[:, 0, 0:1], waT[0:2, :], a2[0:2, :], start=True, stop=True).then_inc(g_mm, 1)
        pe.wait_ge(g_cp, 1)
        nc.tensor.matmul(ps1[:, 0, 1:2], wTt, wa2, start=True, stop=True).then_inc(g_mm, 1)
        pe.wait_ge(wsq_done, 2)
        pe.wait_ge(vec_consts, 3)
        nc.tensor.matmul(ps1[:, 1, 0:2 * D], ones, wsq, start=True, stop=True).then_inc(g_mm, 1)
        pe.wait_ge(pool_consts, 2)
        pe.wait_ge(g_cp, 2)
        for g in range(17):
            if g < 16:
                pe.wait_ge(normed, g // 4 + 1)
                if g >= 2:
                    pe.wait_ge(hT_done, g - 1)
                for b in range(4):
                    last = nc.tensor.transpose(setT[g % 2][:, b * P:(b + 1) * P], X[:, 4 * g + b, :], ident[:, :])
                last.then_inc(tr_done, 1)
            if g:
                k = g - 1
                pe.wait_ge(hT_done, k + 1)
                if k >= 2:
                    pe.wait_ge(hp_cp, k - 1)
                for b in range(4):
                    last = nc.tensor.matmul(setH[k % 2][:, b // 2, (b % 2) * (D + 1):(b % 2 + 1) * (D + 1)],
                                            hT[k % 2][:, b * P:(b + 1) * P], wG, start=(b % 2 == 0), stop=(b % 2 == 1),
                                            skip_group_check=True)
                last.then_inc(hp_mm, 1)
        pe.wait_ge(hb_done, 1)
        nc.tensor.matmul(ps1[:, 0, 128:256], hb, wG[:, 0:D], start=True, stop=True).then_inc(mean_mm, 1)
        pe.wait_ge(hp_cp, 16)
        pe.wait_ge(v0_cols, 1)
        pe.wait_ge(mean_cp, 1)

        def chunk(s, c):
            n = CH * s + c
            pe.wait_ge(mask_ready, n + 1)
            for t in range(CT):
                k = CT * c + t
                for b in range(BL):
                    last = nc.tensor.matmul(ps0[:, b, 0:NV0], mask[:, c % NMASK, t * IW + b * P:t * IW + (b + 1) * P],
                                            V0[:, k, :], start=(k == 0), stop=(k == T - 1))
            last.then_inc(l0_done, 1)

        def octet(sums, count, o, begin, end):
            pe.wait_ge(unpacked, count + 1)
            for t in range(OCT):
                for b in range(BL):
                    last = nc.tensor.matmul(sums[:, b // 2, (b % 2) * 2 * D:(b % 2 + 1) * 2 * D],
                                            unp[:, o % 2, b % 2, t * 256 + (b // 2) * P:t * 256 + (b // 2 + 1) * P],
                                            V1[:, OCT * o + t, :], start=(begin and t == 0 and b % 2 == 0),
                                            stop=(end and t == OCT - 1), skip_group_check=True)
            return last

        def rows(e, after):
            if after == 5:
                pe.wait_ge(h_ready, e + 1)
                for b in range(BL):
                    last = nc.tensor.transpose(psT[:, b * P:(b + 1) * P], num[:, b, :], ident[:, :])
                last.then_inc(rowT_done, 1)
            if after == 7:
                pe.wait_ge(rowT_copied, e + 1)
                wait(pe, v_ready, e)
                for b in range(BL):
                    last = nc.tensor.matmul(psH[:, b * P:(b + 1) * P], ev[:, b, 0:D], WT[:, :],
                                            start=(b == 0), stop=(b == BL - 1), skip_group_check=True)
                last.then_inc(rowW_done, 1)

        def body(s, first, octets):
            for c in range(CH):
                if c == 0:
                    if isinstance(s, int) and s == 0:
                        pe.wait_ge(v0_lo, 4)
                    else:
                        pe.wait_ge(ev_ready, s)
                chunk(s, c)
                if not (isinstance(s, int) and s == 0):
                    rows(s - 1, c)
                half = octets // 2
                for o in {7: range(half), 11: range(half, octets)}.get(c, ()):
                    if o == 0 and not (isinstance(s, int) and s <= FIRST_L1):
                        pe.wait_ge(l1_sum, s - FIRST_L1)
                    pe.wait_ge(v1_ready, 2 * o + 2)
                    octet(ps1, octets_before(s, first, octets) + o, o, o == 0, o == octets - 1).then_inc(l1_octet, 1)

        superblocks(pe, body)
        for c in range(CH):
            rows(SB - 1, c)

        count = EARLY
        for s in range(SB):
            wait(pe, tail_sum, s - 1)
            if s == 0:
                pe.wait_ge(ev_ready, SB)
            for b in range(BL):
                if s == SB - 1 or s == 0:
                    pe.wait_ge(v1_ready, s + 1)
                nc.tensor.matmul(tail_ps(s)[:, b // 2, (b % 2) * 2 * D:(b % 2 + 1) * 2 * D], ident2[:, :],
                                 V1[:, BL * s + b, :], start=(b % 2 == 0), stop=False, skip_group_check=True)
            for o in range(OCTETS[s], SB // 2):
                if o == SB // 2 - 1:
                    pe.wait_ge(v1_ready, SB)
                last = octet(tail_ps(s), count, o, False, o == SB // 2 - 1)
                last.then_inc(l1_octet, 1)
                count += 1

    @block.vector
    def _(dve):
        steps = [0]

        def link(ins):
            steps[0] += 1
            ins.then_inc(vec_step, 1)
            dve.wait_ge(vec_step, steps[0])

        nc.vector.memset(ones, 1.0).then_inc(vec_consts, 1)
        nc.vector.memset(epsc, EPS).then_inc(vec_consts, 1)
        dve.wait_ge(pool_consts, 2)
        nc.vector.tensor_scalar(ident2[:, :], ident[:, :], 2.0, None, ALU.mult).then_inc(vec_consts, 1)
        dve.wait_ge(weights_in, 96)
        nc.vector.tensor_tensor(wsq[:, 0:D], wG[:, 0:D], wG[:, 0:D], ALU.mult).then_inc(wsq_done, 1)
        nc.vector.tensor_tensor(wsq[:, D:2 * D], WT[:, :], WT[:, :], ALU.mult).then_inc(wsq_done, 1)
        dve.wait_ge(g_mm, 1)
        nc.vector.tensor_copy(wa2, ps1[:, 0, 0:1]).then_inc(g_cp, 1)
        dve.wait_ge(g_mm, 2)
        nc.vector.tensor_copy(wG[:, D:D + 1], ps1[:, 0, 1:2]).then_inc(g_cp, 1)
        dve.wait_ge(g_mm, 3)
        for k in range(2):
            link(nc.vector.tensor_reduce(cmax[:, k:k + 1], ps1[:, 1, k * D:(k + 1) * D], AX.X, ALU.max))
        nc.vector.tensor_scalar(cmax, cmax, 1e-30, None, ALU.max).then_inc(norms_done, 1)

        def normalise(q):
            dve.wait_ge(std_done, q + 1)
            link(nc.vector.reciprocal(rstd[:, 16 * q:16 * q + 16], sd[:, 16 * q:16 * q + 16]))
            for t in range(16 * q, 16 * q + 16):
                last = nc.vector.tensor_scalar(X[:, t, :], X[:, t, :], mv[:, t, 0:1], rstd[:, t:t + 1],
                                               ALU.subtract, ALU.mult)
            last.then_inc(normed, 1)

        for q in range(4):
            dve.wait_ge(x_part[q], 16)
            for t in range(16 * q, 16 * q + 16):
                last = nc.vector.bn_stats(st[:, t, :], X[:, t, :])
            link(last)
            for t in range(16 * q, 16 * q + 16):
                last = nc.vector.bn_aggr(mv[:, t, :], st[:, t, :])
            last.then_inc(var_done, 1)
            if q:
                normalise(q - 1)
        normalise(3)

        dve.wait_ge(norm_sqrt, 1)
        link(nc.vector.reciprocal(sig[:, 6:8], cmax))
        link(nc.vector.tensor_scalar(sig[:, 6:8], sig[:, 6:8], BOUND, None, ALU.mult))
        link(nc.vector.tensor_scalar(sig[:, 0:2].bitcast(U32), sig[:, 6:8].bitcast(U32), 0x7F800000, None,
                                     ALU.bitwise_and))
        link(nc.vector.tensor_scalar(sig[:, 2:3], sig[:, 0:1], 1.0 / M_SCALE, None, ALU.mult))
        link(nc.vector.reciprocal(sig[:, 3:4], sig[:, 1:2]))
        link(nc.vector.tensor_scalar(sig[:, 4:5], sig[:, 3:4], 0.5, None, ALU.mult))

        dve.wait_ge(hT_done, 16)
        link(nc.vector.reduce_sum(hsum1, hsum, AX.X))
        nc.vector.tensor_scalar(hb, ones, hsum1, 1.0 / N, ALU.mult, ALU.mult).then_inc(hb_done, 1)
        dve.wait_ge(mean_mm, 1)
        nc.vector.tensor_scalar(meanh[:, :], ps1[:, 0, 128:256], 0.0, None, ALU.max).then_inc(mean_cp, 1)

        dve.wait_ge(hp_cp, 16)
        link(nc.vector.tensor_scalar(kf, f, LOG2E, ROUND, ALU.mult, ALU.add))
        link(nc.vector.tensor_scalar(kf, kf, -ROUND, None, ALU.add))
        nc.vector.tensor_reduce(kmax, kf, AX.X, ALU.max).then_inc(kmax_done, 1)
        link(nc.vector.scalar_tensor_tensor(r1, kf, -LN2_HI, f, ALU.mult, ALU.add))
        nc.vector.scalar_tensor_tensor(r1, kf, -LN2_LO, r1, ALU.mult, ALU.add).then_inc(frac_done, 1)
        dve.wait_ge(kall_done, 1)
        link(nc.vector.tensor_scalar(ke, kf, kall, float(TOP), ALU.subtract, ALU.add))
        link(nc.vector.tensor_scalar(ke, ke, float(LOW), None, ALU.max))
        link(nc.vector.tensor_scalar(sbit, ke, 127.0, float(2 ** 23), ALU.add, ALU.mult))
        link(nc.vector.tensor_copy(scale2[:, :].bitcast(I32), sbit))
        dve.wait_ge(exp_done, 1)
        nc.vector.tensor_scalar(mS, m, sig[:, 0:1], None, ALU.mult).then_inc(vec_step, 1)
        steps[0] += 1
        link(nc.vector.tensor_scalar(m, m, M_SCALE, None, ALU.mult))
        for q in range(4):
            sl = slice(16 * q, 16 * q + 16)
            nc.vector.tensor_tensor(H[:, sl, :], H[:, sl, :], wide(mS[:, sl]), ALU.mult).then_inc(v0_f32, 1)
        link(nc.vector.tensor_copy(V0[:, :, 2 * D], m))
        nc.vector.tensor_tensor(V0[:, :, 2 * D + 1], m, V0[:, :, 2 * D], ALU.subtract)
        for b in range(BUCKETS):
            link(nc.vector.tensor_scalar(w15[b], ke, -1.0, float(TOP - 14 - 30 * b + 15), ALU.mult, ALU.add))
            link(nc.vector.scalar_tensor_tensor(q1[b], w15[b], 1.0, w15[b], ALU.is_ge, ALU.mult))
            link(nc.vector.scalar_tensor_tensor(q2[b], w15[b], 30.0, q1[b], ALU.is_le, ALU.mult))
            last = nc.vector.tensor_scalar(V0[:, :, 2 * D + 2 + b].bitcast(U16), q2[b], 1024.0, None, ALU.mult)
        last.then_inc(v0_cols, 1)
        setup_steps = steps[0]

        def pack(s, c, read):
            if c < 2:
                return
            if read is not None:
                dve.wait_ge(unpacked, read)
            dve.wait_ge(byte_ready, CH * s + c + 1)
            if c >= 4:
                dve.wait_ge(packed, 14 * s + (c - 2) - 1)
            dst = bits[:, s, (c % 2) * CT * IW:(c % 2 + 1) * CT * IW].bitcast(U32)
            nc.vector.scalar_tensor_tensor(dst, byte[:, c % 2, :].bitcast(U32), c // 2, dst,
                                           ALU.logical_shift_left, ALU.bitwise_or).then_inc(packed, 1)

        def unpack(s, o, free):
            wait(dve, l1_octet, free)
            for par in range(2):
                shift = 14 - o - 8 * par
                last = nc.vector.tensor_scalar(
                    unp[:, o % 2, par, :].bitcast(U32), bits[:, s, :].bitcast(U32), abs(shift), 0x40004000,
                    ALU.logical_shift_left if shift >= 0 else ALU.logical_shift_right, ALU.bitwise_and)
            last.then_inc(unpacked, 1)

        def rows(e, after):
            def step(ins, k):
                ins.then_inc(row_step, 1)
                dve.wait_ge(row_step, ROW_STEPS * e + k)

            if after == 1:
                dve.wait_ge(ev_ready, e + 1)
                wait(dve, v1_ready, e)
                nc.vector.tensor_tensor(cprod[:, :, :], ev[:, :, 2 * D + 2:NV0],
                                        cw[:, :].unsqueeze(1).broadcast_to([P, BL, BUCKETS]), ALU.mult)
                step(nc.vector.tensor_tensor(den[:, :], ev[:, :, 2 * D], ev[:, :, 2 * D + 1], ALU.add), 1)
                step(nc.vector.tensor_reduce(cnt[:, :], cprod[:, :, :], AX.X, ALU.add), 2)
                nc.vector.tensor_tensor(num[:, :, :], ev[:, :, 0:D], ev[:, :, D:2 * D], ALU.add)
                step(nc.vector.tensor_scalar(zero_row[:, :], cnt[:, :], 0.0, None, ALU.is_equal), 3)
                nc.vector.scalar_tensor_tensor(den[:, :], den[:, :], sig[:, 2:3], zero_row[:, :], ALU.mult,
                                               ALU.add).then_inc(z_ready, 1)
                dve.wait_ge(z_ready, e + 1)
                step(nc.vector.reciprocal(rden[:, :], den[:, :]), 4)
                step(nc.vector.tensor_tensor(num[:, :, :], num[:, :, :], wide(rden[:, :]), ALU.mult), 5)
                dve.wait_ge(xz_ready, e + 1)
                nc.vector.scalar_tensor_tensor(xb[:, :, :], num[:, :, :], 0.0, xb[:, :, :], ALU.max,
                                               ALU.add).then_inc(x1_ready, 1)
            if after == 2:
                dve.wait_ge(x1_ready, e + 1)
                for b in range(BL):
                    last = nc.vector.bn_stats(bst[:, b, :], xb[:, b, :])
                last.then_inc(rstat_done, 1)
                dve.wait_ge(rstat_done, 2 * e + 1)
                nc.vector.tensor_scalar(sq[:, BL:2 * BL], cnt[:, :], 1.0, None, ALU.add)
                for b in range(BL):
                    last = nc.vector.bn_aggr(bmv[:, b, :], bst[:, b, :])
                last.then_inc(rstat_done, 1)
                dve.wait_ge(rstat_done, 2 * e + 2)
                nc.vector.tensor_scalar(sq[:, 0:BL], bmv[:, :, 1], EPS, None, ALU.add).then_inc(sq_ready, 1)
            if after == 3:
                dve.wait_ge(sqrt_done, e + 1)
                nc.vector.reciprocal(rs[:, :], rs[:, :]).then_inc(rs_recip, 1)
                dve.wait_ge(rs_recip, e + 1)
                nc.vector.scalar_tensor_tensor(nbias[:, :], bmv[:, :, 0], -1.0, rs[:, 0:BL], ALU.mult, ALU.mult)
                nc.vector.tensor_copy(dalls[:, e, :], rs[:, BL:2 * BL])
                nc.vector.tensor_scalar(dsig[:, :], rs[:, BL:2 * BL], sig[:, 1:2], None, ALU.mult)
                nc.vector.tensor_scalar(dback[:, :], rs[:, BL:2 * BL], sig[:, 4:5], None,
                                        ALU.mult).then_inc(rs_ready, 1)
            if after == 5 and not (isinstance(e, int) and e < FIRST_L1):
                dve.wait_ge(l1_low, e - FIRST_L1 + 1)
                part = ev[:, :, D:2 * D].rearrange("p (a b) f -> p a b f", b=2)
                nc.vector.tensor_tensor(part, ps1[:, :, :].rearrange("p a (b f) -> p a b f", b=2)[:, :, :, 0:D],
                                        part, ALU.add).then_inc(l1_sum, 1)
            if after == 9:
                dve.wait_ge(rowW_done, e + 1)
                dve.wait_ge(rs_ready, e + 1)
                nc.vector.tensor_tensor(num[:, :, :], psH[:, :].rearrange("p (b f) -> p b f", b=BL),
                                        wide(dsig[:, :]), ALU.mult).then_inc(v_ready, 1)

        def body(s, first, octets):
            half = octets // 2
            place = {7 + k: k for k in range(half)}
            place.update({11 + k - half: k for k in range(half, octets)})
            for c in range(CH):
                n = CH * s + c
                dve.wait_ge(adj_landed[c % NSTAGE], 4 * 16 * s + 16 * (c // NSTAGE + 1))
                wait(dve, l0_done, n - NMASK + 1)
                for t in range(CT):
                    k = CT * c + t
                    last = nc.vector.tensor_scalar(mask[:, c % NMASK, t * IW:(t + 1) * IW],
                                                   stage[:, c % NSTAGE, t * IW:(t + 1) * IW], 0.0,
                                                   scale2[:, k:k + 1], ALU.is_gt, ALU.mult)
                last.then_inc(mask_ready, 1)
                pack(s, c, octets_before(s, first, octets) + place[c - 1] + 1 if c - 1 in place else None)
                if not (isinstance(s, int) and s == 0):
                    rows(s - 1, c)
                if c in place:
                    o = place[c]
                    before = octets_before(s, first, octets)
                    dve.wait_ge(packed, 14 * s + c - 1)
                    unpack(s, o, before + (o - 1 if o >= 2 else 0))

        superblocks(dve, body)
        for c in range(CH):
            rows(SB - 1, c)

        dve.wait_ge(rs_ready, SB)
        dve.wait_ge(packed, 14 * SB)
        nc.vector.tensor_scalar(dall[:, :], dall[:, :], sig[:, 4:5], None, ALU.mult).then_inc(dall_done, 1)

        def finish(s):
            ybuf = [xb, num][s % 2]
            part = tail_part(s)
            part4 = part.rearrange("p (a b) f -> p a b f", b=2)
            dve.wait_ge(tail_low, s + 1)
            nc.vector.tensor_tensor(part4, tail_ps(s).rearrange("p a (b f) -> p a b f", b=2)[:, :, :, 0:D], part4,
                                    ALU.add).then_inc(tail_sum, 1)
            dve.wait_ge(tail_sum, s + 1)
            dve.wait_ge(dall_done, 1)
            nc.vector.tensor_tensor(part, part, wide(dalls[:, s, :]), ALU.mult).then_inc(tail_scaled, 1)
            dve.wait_ge(tail_scaled, s + 1)
            dve.wait_ge(tail_x[s % 2], 16 * (s // 2 + 1))
            nc.vector.tensor_tensor(ybuf[:, :, :], ybuf[:, :, :], part, ALU.add).then_inc(tail_out, 1)

        count = EARLY
        users = {0: EARLY, 1: EARLY}
        for s in range(SB):
            for o in range(OCTETS[s], SB // 2):
                unpack(s, o, users[o % 2])
                count += 1
                users[o % 2] = count
                if o == OCTETS[s] and s:
                    finish(s - 1)
        finish(SB - 1)

    ctx.close()


_INS = [("adj", (SB, CH, P, CT * IW)), ("x", (P, SB, BL, D)), ("w", (D, D)), ("wT", (D, D)), ("waT", (2, D)),
        ("a", (2, 1)), ("WT", (D, D)), ("b", (P, D))]


def kernel(x, adj, L0_gnn_w, L0_gnn_w_a, L0_gnn_a, L1_gnn_W, L1_gnn_b):
    import concourse.bacc as bacc
    from concourse.bass_utils import run_bass_kernel_spmd

    x, adj, w, w_a, a, W, b = (np.asarray(v) for v in (x, adj, L0_gnn_w, L0_gnn_w_a, L0_gnn_a, L1_gnn_W, L1_gnn_b))
    chunks = adj.reshape(SB, IW, CH, CT, P).transpose(0, 2, 4, 3, 1).reshape(SB, CH, P, CT * IW)
    arrays = {
        "adj": np.ascontiguousarray(chunks),
        "x": np.ascontiguousarray(x.reshape(T, P, D).transpose(1, 0, 2)).reshape(P, SB, BL, D),
        "w": np.ascontiguousarray(w),
        "wT": np.ascontiguousarray(w.T),
        "waT": np.ascontiguousarray(w_a.T),
        "a": np.ascontiguousarray(a[2:4]),
        "WT": np.ascontiguousarray(W.T),
        "b": np.ascontiguousarray(np.broadcast_to(b[None, :], (P, D))),
    }
    nc = bacc.Bacc("TRN2", target_bir_lowering=False, num_devices=1, dynamic_dma_scratch_size=1024)
    ins = [nc.dram_tensor(f"{name}_in", shape, F32, kind="ExternalInput").ap() for name, shape in _INS]
    out = nc.dram_tensor("out", (P, SB, BL, D), F32, kind="ExternalOutput").ap()
    build(nc, ins, out)
    r = run_bass_kernel_spmd(nc, [{f"{k}_in": v for k, v in arrays.items()}], core_ids=[0])
    got = r.results[0]["out"]
    return np.ascontiguousarray(got.reshape(P, T, D).transpose(1, 0, 2)).reshape(N, D)
```

```python
from contextlib import ExitStack
import math

import numpy as np
import concourse.bass as bass
from concourse import mybir

F32, F16, BF16 = mybir.dt.float32, mybir.dt.float16, mybir.dt.bfloat16
U8, U16, U32, I32 = mybir.dt.uint8, mybir.dt.uint16, mybir.dt.uint32, mybir.dt.int32
ALU = mybir.AluOpType
ACT = mybir.ActivationFunctionType
AX = mybir.AxisListType

P = 128
N = 8192
D = 128
T = N // P
BL = 4
SB = T // BL
IW = BL * P
CT = 4
CH = T // CT
OCT = 8
NSTAGE = 4
NMASK = 4
EPS = 1e-5

LOG2E = float(np.float32(1.0 / math.log(2.0)))
LN2_HI = float(np.float32(0.693359375))
LN2_LO = float(np.float32(math.log(2.0) - 0.693359375))
ROUND = float(3 << 22)
TOP = 60
BUCKETS = 4
LOW = TOP - 30 * BUCKETS + 1
M_SCALE = 1024.0
NV0 = 2 * D + 2 + BUCKETS
BOUND = 2.0 ** 14 / (math.sqrt(D) * 1.42)

GROUPS = [(0, 1, 0), (1, 1, 0), (2, 1, 1), (3, 1, 1)] + [(2 * p, 2, p) for p in range(2, SB // 2)]
EARLY = [(e + 1) // 2 for e in range(SB - 1)] + [0]
FIRST_L1 = 1
ROW_STEPS = 5

PLACES = {0: [], 1: [13], 2: [-1, 13], 3: [-1, 7, 13], 4: [-1, 3, 7, 13], 5: [-1, 3, 7, 10, 13],
          6: [-1, 3, 3, 7, 10, 13], 7: [-1, 3, 3, 7, 7, 11, 13]}
ROW_PLACES = {
    "act": [dict(evac=0, low=1, sqrt=2, relu=3, store=4, turn=6, high=9),
            dict(evac=2, low=1, sqrt=4, relu=5, store=6, turn=8, high=12)],
    "dve": [dict(low=1, sums=1, stats=2, scales=3, v=9), dict(low=1, sums=2, stats=3, scales=4, v=11)],
    "pe": [dict(turn=5, weigh=7), dict(turn=5, weigh=7)],
}


LATE = 2


def row_parts(engine, octets, c):
    return [k for k, at in ROW_PLACES[engine][octets >= LATE].items() if at == c]


LATE_OCTETS = [(s, o) for s in range(SB) for o in range(EARLY[s], SB // 2)]


def row_order(engine):
    return sorted(ROW_PLACES[engine][0], key=ROW_PLACES[engine][0].get)


def octets_before(s, first, octets):
    return sum(k // 2 for k in range(first)) + (s - first) * octets


def octets_through_late(s):
    return sum(EARLY) + sum(SB // 2 - o for o in EARLY[:s + 1])


def build(nc, ins, outs):
    adj, x_in, w_in, wT_in, waT_in, a_in, WT_in, b_in = ins
    out = outs
    y_dram = nc.dram_tensor("y_scratch", (P, SB, BL, D), F32, kind="Internal").ap()
    ctx = ExitStack()

    def sb(name, shape, dt):
        return ctx.enter_context(nc.sbuf_tensor(name, shape, dt))

    def sem(name):
        return ctx.enter_context(nc.semaphore(name))

    bits = sb("bits", [P, SB, OCT * IW], U8)
    V0 = sb("V0", [P, T, NV0], F16)
    V1 = sb("V1", [P, T, 2 * D], F16)
    stage = sb("stage", [P, NSTAGE, CT * IW], F32)
    mask = sb("mask", [P, NMASK, CT * IW], BF16)
    byte = sb("byte", [P, 2, CT * IW], U8)
    unp = sb("unp", [P, 2, 2, OCT * IW // 2], F16)
    ev = sb("ev", [P, BL, NV0], F32)
    num = sb("num", [P, BL, D], F32)
    xb = sb("xb", [P, BL, D], F32)
    yb = sb("yb", [P, BL, D], F32)
    low = sb("low", [P, BL, D], F32)
    ident = sb("ident", [P, P], F32)
    ident2 = sb("ident2", [P, P], F16)
    WT = sb("WT", [P, D], F32)
    bias = sb("bias", [P, D], F32)
    meanh = sb("meanh", [P, D], F32)
    scale2 = sb("scale2", [P, T], F32)
    dall = sb("dall", [P, T], F32)
    sig = sb("sig", [P, 8], F32)
    cw = sb("cw", [P, BUCKETS], F32)
    den = sb("den", [P, BL], F32)
    cprod = sb("cprod", [P, BL, BUCKETS], F32)
    zero_row = sb("zero_row", [P, BL], F32)
    cnt = sb("cnt", [P, BL], F32)
    rden = sb("rden", [P, BL], F32)
    bst = sb("bst", [P, BL, 6], F32)
    bmv = sb("bmv", [P, BL, 2], F32)
    sq = sb("sq", [P, 2 * BL], F32)
    rs = sb("rs", [P, 2 * BL], F32)
    nbias = sb("nbias", [P, BL], F32)
    dsig = sb("dsig", [P, BL], F32)
    dback = sb("dback", [P, BL], F32)
    zcol = sb("zcol", [P, 1], F32)

    low_half = bits[:, 0:SB // 2, :].rearrange("p s n -> p (s n)").bitcast(F32)
    high_half = bits[:, SB // 2:SB, :].rearrange("p s n -> p (s n)").bitcast(F32)
    H = low_half.rearrange("p (t f) -> p t f", f=D)
    X = high_half.rearrange("p (t f) -> p t f", f=D)
    v1f = V1[:, :, :].rearrange("p t f -> p (t f)").bitcast(F32)
    hT = [v1f[:, 512 * k:512 * k + 512] for k in range(2)]
    at = [1024]

    def small(n):
        a = at[0]
        at[0] += n
        return v1f[:, a:a + n]

    ones = small(P)
    wG = small(D + 1)
    wTt = small(D)
    waT = small(D)
    a2 = small(1)
    wa2 = small(1)
    wsq = small(2 * D)
    cmax = small(2)
    st = small(T * 6).rearrange("p (t k) -> p t k", k=6)
    mv = small(T * 2).rearrange("p (t k) -> p t k", k=2)
    sd = small(T)
    rstd = small(T)
    epsc = small(1)
    f = small(T)
    kf = small(T)
    r1 = small(T)
    m = small(T)
    mS = small(T)
    kmax = small(1)
    kall = small(1)
    ke = small(T)
    sbit = small(T).bitcast(I32)
    w15 = [small(T) for _ in range(BUCKETS)]
    q1 = [small(T) for _ in range(BUCKETS)]
    q2 = [small(T) for _ in range(BUCKETS)]

    ps0 = ctx.enter_context(nc.psum_tensor("ps0", [P, BL, 512], F32))
    ps1 = ctx.enter_context(nc.psum_tensor("ps1", [P, 2, 512], F32))
    psT = ctx.enter_context(nc.psum_tensor("psT", [P, 512], F32))
    psH = ctx.enter_context(nc.psum_tensor("psH", [P, 512], F32))
    setT = [psT, psH]
    setH = [ps0[:, 0:2, :], ps0[:, 2:4, :]]

    weights_in = sem("weights_in")
    x_part = [sem(f"x_part{q}") for q in range(4)]
    pool_consts = sem("pool_consts")
    vec_consts = sem("vec_consts")
    std_done = sem("std_done")
    g_mm = sem("g_mm")
    g_cp = sem("g_cp")
    tr_done = sem("tr_done")
    hT_done = sem("hT_done")
    hp_mm = sem("hp_mm")
    hp_cp = sem("hp_cp")
    hp_cp2 = sem("hp_cp2")
    centred = sem("centred")
    norm_sqrt = sem("norm_sqrt")
    mean_mm = sem("mean_mm")
    mean_cp = sem("mean_cp")
    rstd_done = sem("rstd_done")
    var_done = sem("var_done")
    norms_done = sem("norms_done")
    wsq_done = sem("wsq_done")
    frac_done = sem("frac_done")
    kmax_done = sem("kmax_done")
    v0_cols = sem("v0_cols")
    vec_step = sem("vec_step")
    exp_done = sem("exp_done")
    kall_done = sem("kall_done")
    v0_f32 = sem("v0_f32")
    v0_hi = sem("v0_hi")
    v0_lo = sem("v0_lo")
    adj_landed = [sem(f"adj_landed{k}") for k in range(NSTAGE)]
    mask_ready = sem("mask_ready")
    byte_ready = sem("byte_ready")
    packed = sem("packed")
    l0_done = sem("l0_done")
    unpacked = sem("unpacked")
    l1_octet = sem("l1_octet")
    x_loaded = sem("x_loaded")
    ev_ready = sem("ev_ready")
    row_step = sem("row_step")
    z_ready = sem("z_ready")
    xz_ready = sem("xz_ready")
    x1_ready = sem("x1_ready")
    sq_ready = sem("sq_ready")
    sqrt_done = sem("sqrt_done")
    rs_ready = sem("rs_ready")
    h_ready = sem("h_ready")
    rowT_done = sem("rowT_done")
    rowT_copied = sem("rowT_copied")
    rowW_done = sem("rowW_done")
    v_ready = sem("v_ready")
    v1_hi = sem("v1_hi")
    v1_ready = sem("v1_ready")
    l1_low = sem("l1_low")
    l1_scaled = sem("l1_scaled")
    biased = sem("biased")
    zrow_done = sem("zrow_done")
    rstat_done = sem("rstat_done")
    rs_recip = sem("rs_recip")
    dall_done = sem("dall_done")
    l1_sum = sem("l1_sum")
    y_ready = sem("y_ready")
    y_stored = sem("y_stored")
    tail_x = [sem(f"tail_x{k}") for k in range(2)]
    tail_low = sem("tail_low")
    tail_sum = sem("tail_sum")
    tail_scaled = sem("tail_scaled")
    tail_out = sem("tail_out")
    out_stored = [sem(f"out_stored{k}") for k in range(2)]

    def wait(eng, s, value):
        if not isinstance(value, int) or value > 0:
            eng.wait_ge(s, value)

    def superblocks(eng, body):
        for first, count, octets in GROUPS:
            if count == 1:
                body(first, first, octets)
            else:
                with eng.Fori(first, first + count) as s:
                    body(s, first, octets)

    def wide(v):
        return v.unsqueeze(2).broadcast_to([P, v.shape[1], D])

    def per_block(v):
        return v.unsqueeze(1).broadcast_to([P, BL, D])

    def tail_ps(s):
        return ps0[:, 2 * (s % 2):2 * (s % 2) + 2, :]

    def tail_part(s):
        return ev[:, :, D * (s % 2):D * (s % 2) + D]

    def copy_products(copy, g):
        src = setH[g % 2][:, :, 0:2 * (D + 1)].rearrange("p a (b f) -> p a b f", b=2)
        copy(H[:, 4 * g:4 * g + 4, :].rearrange("p (a b) f -> p a b f", b=2), src[:, :, :, 0:D])
        copy(f[:, 4 * g:4 * g + 4].rearrange("p (a b) -> p a b", b=2), src[:, :, :, D]).then_inc(
            hp_cp if g < 8 else hp_cp2, 1)

    V1s = V1[:, :, :].rearrange("p (s b) f -> p s b f", b=BL)
    dalls = dall[:, :].rearrange("p (s b) -> p s b", b=BL)

    block = ctx.enter_context(nc.Block())

    @block.sync
    def _(sp):
        for q in range(4):
            sp.dma_start(X[:, 16 * q:16 * q + 16, :],
                         x_in[:, 4 * q:4 * q + 4].rearrange("p s b f -> p (s b) f")).then_inc(x_part[q], 16)
            if q == 0:
                for dst, src in [(wG[:, 0:D], w_in), (wTt, wT_in), (waT[0:2, :], waT_in), (a2[0:2, :], a_in),
                                 (WT[:, :], WT_in), (bias[:, :], b_in)]:
                    sp.dma_start(dst, src).then_inc(weights_in, 16)

        def body(s, first, octets):
            for c in range(CH):
                n = CH * s + c
                wait(sp, mask_ready, n - NSTAGE + 1)
                wait(sp, byte_ready, n - NSTAGE + 1)
                sp.dma_start(stage[:, c % NSTAGE, :], adj[s, c]).then_inc(adj_landed[c % NSTAGE], 16)
                if c == 13:
                    wait(sp, biased, s)
                    sp.dma_start(xb[:, :, :], x_in[:, s]).then_inc(x_loaded, 16)

        superblocks(sp, body)

        for s in range(SB + 2):
            if s < SB:
                if s == 0:
                    sp.wait_ge(y_stored, 16 * SB)
                    sp.wait_ge(v1_ready, SB)
                if s >= 2:
                    sp.wait_ge(out_stored[s % 2], 16 * (s // 2))
                sp.dma_start([xb, num][s % 2][:, :, :], y_dram[:, s]).then_inc(tail_x[s % 2], 16)
            if 1 <= s <= SB:
                sp.wait_ge(tail_out, s)
                sp.dma_start(out[:, s - 1], [xb, num][(s - 1) % 2][:, :, :]).then_inc(out_stored[(s - 1) % 2], 16)
        for k in range(2):
            sp.wait_ge(out_stored[k], 16 * SB // 2)

    @block.gpsimd
    def _(pool):
        nc.gpsimd.memset(ident[:], 0.0).then_inc(pool_consts, 1)
        pool.wait_ge(pool_consts, 1)
        nc.gpsimd.affine_select(out=ident[:], in_=ident[:], compare_op=ALU.not_equal, fill=1.0, base=0,
                                pattern=[[-1, P]], channel_multiplier=1).then_inc(pool_consts, 1)
        for b in range(BUCKETS):
            nc.gpsimd.memset(cw[:, b:b + 1], 2.0 ** -(TOP - 14 - 30 * b)).then_inc(pool_consts, 1)
        for q in range(4):
            pool.wait_ge(var_done, q + 1)
            nc.gpsimd.tensor_tensor(X[:, 16 * q:16 * q + 16, :], X[:, 16 * q:16 * q + 16, :],
                                    mv[:, 16 * q:16 * q + 16, 0].unsqueeze(2).broadcast_to([P, 16, D]),
                                    ALU.subtract).then_inc(centred, 1)
        pool.wait_ge(kmax_done, 1)
        nc.gpsimd.partition_all_reduce(kall, kmax, P, bass.bass_isa.ReduceOp.max).then_inc(kall_done, 1)

        for q in range(4):
            pool.wait_ge(v0_hi, q + 1)
            nc.gpsimd.tensor_tensor(V0[:, 16 * q:16 * q + 16, D:2 * D], X[:, 16 * q:16 * q + 16, :],
                                    V0[:, 16 * q:16 * q + 16, 0:D], ALU.subtract).then_inc(v0_lo, 1)

        def rows(s):
            e = s - 1
            if not (isinstance(s, int) and s - 2 < FIRST_L1):
                pool.wait_ge(l1_sum, s - 2)
                nc.gpsimd.tensor_tensor(low[:, :, :], low[:, :, :], wide(dback[:, :]), ALU.mult).then_inc(l1_scaled, 1)
                pool.wait_ge(l1_scaled, s - 2)
                nc.gpsimd.tensor_tensor(yb[:, :, :], yb[:, :, :], low[:, :, :], ALU.add).then_inc(y_ready, 1)
            pool.wait_ge(z_ready, e + 1)
            if isinstance(s, int):
                pool.wait_ge(mean_cp, 1)
            nc.gpsimd.tensor_tensor(ev[:, :, 0:D], wide(zero_row[:, :]), per_block(meanh[:, :]),
                                    ALU.mult).then_inc(zrow_done, 1)
            pool.wait_ge(x_loaded, 16 * (e + 1))
            pool.wait_ge(zrow_done, e + 1)
            nc.gpsimd.tensor_tensor(xb[:, :, :], xb[:, :, :], ev[:, :, 0:D], ALU.add).then_inc(xz_ready, 1)
            pool.wait_ge(h_ready, e + 1)
            wait(pool, y_stored, 16 * e)
            nc.gpsimd.tensor_tensor(yb[:, :, :], xb[:, :, :], per_block(bias[:, :]), ALU.add).then_inc(biased, 1)
            pool.wait_ge(v1_hi, e + 1)
            nc.gpsimd.tensor_tensor(V1s[:, e, :, D:2 * D], num[:, :, :], V1s[:, e, :, 0:D],
                                    ALU.subtract).then_inc(v1_ready, 1)

        rows(1)
        rows(2)
        with pool.Fori(3, SB + 1) as s:
            rows(s)

    @block.scalar
    def _(act):
        act.wait_ge(vec_consts, 3)
        for g in range(16):
            act.wait_ge(tr_done, g + 1)
            if g >= 2:
                act.wait_ge(hp_mm, g - 1)
            nc.scalar.activation(hT[g % 2], setT[g % 2][:, :], ACT.Relu).then_inc(hT_done, 1)
            if 1 <= g <= 8:
                act.wait_ge(hp_mm, g)
                copy_products(nc.scalar.copy, g - 1)
        act.wait_ge(var_done, 4)
        nc.scalar.activation(sd, mv[:, :, 1], ACT.Sqrt, bias=epsc).then_inc(std_done, 1)
        act.wait_ge(norms_done, 1)
        nc.scalar.activation(cmax, cmax, ACT.Sqrt).then_inc(norm_sqrt, 1)
        act.wait_ge(frac_done, 1)
        nc.scalar.activation(m, r1, ACT.Exp).then_inc(exp_done, 1)

        def high_parts(q):
            sl = slice(16 * q, 16 * q + 16)
            act.wait_ge(v0_f32, q + 1)
            nc.scalar.activation(V0[:, sl, 0:D], X[:, sl, :], ACT.Copy).then_inc(v0_hi, 1)

        high_parts(0)

        def rows(s, part, before):
            e = s - 1
            if part == "evac":
                act.wait_ge(l0_done, CH * (e + 1))
                wait(act, rowW_done, e)
                nc.scalar.activation(ev[:, :, :], ps0[:, :, 0:NV0], ACT.Copy).then_inc(ev_ready, 1)
            if part == "low" and not (isinstance(s, int) and s - 2 < FIRST_L1):
                act.wait_ge(l1_octet, before)
                wait(act, y_ready, s - 3)
                nc.scalar.activation(low[:, :, :].rearrange("p (a b) f -> p a b f", b=2),
                                     ps1[:, :, :].rearrange("p a (b f) -> p a b f", b=2)[:, :, :, D:2 * D],
                                     ACT.Copy).then_inc(l1_low, 1)
            if part == "sqrt":
                act.wait_ge(sq_ready, e + 1)
                nc.scalar.activation(rs[:, :], sq[:, :], ACT.Sqrt).then_inc(sqrt_done, 1)
            if part == "relu":
                act.wait_ge(rs_ready, e + 1)
                for b in range(BL):
                    last = nc.scalar.activation(num[:, b, :], xb[:, b, :], ACT.Relu, bias=nbias[:, b:b + 1],
                                                scale=rs[:, b:b + 1])
                last.then_inc(h_ready, 1)
            if part == "store" and not (isinstance(s, int) and s < 2):
                if isinstance(s, int) and s == 2:
                    act.wait_ge(biased, 1)
                else:
                    act.wait_ge(y_ready, s - 2)
                act.dma_start(y_dram[:, s - 2], yb[:, :, :]).then_inc(y_stored, 16)
            if part == "turn":
                act.wait_ge(rowT_done, e + 1)
                nc.scalar.activation(ev[:, :, 0:D], psT[:, :].rearrange("p (b f) -> p b f", b=BL),
                                     ACT.Copy).then_inc(rowT_copied, 1)
            if part == "high":
                act.wait_ge(v_ready, e + 1)
                nc.scalar.activation(V1s[:, e, :, 0:D], num[:, :, :], ACT.Copy).then_inc(v1_hi, 1)

        def body(s, first, octets):
            for c in range(CH):
                n = CH * s + c
                act.wait_ge(adj_landed[c % NSTAGE], 4 * 16 * s + 16 * (c // NSTAGE + 1))
                if isinstance(s, int) and s == 0 and 1 <= c < 4:
                    high_parts(c)
                if c < 2:
                    if isinstance(s, int) and s == 0 and c == 0:
                        act.wait_ge(mean_mm, 1)
                        act.wait_ge(v0_f32, 1)
                    dst = bits[:, s, c * CT * IW:(c + 1) * CT * IW]
                else:
                    wait(act, packed, 14 * s + (c - 2) - 1)
                    dst = byte[:, c % 2, :]
                nc.scalar.activation(dst.rearrange("p (a l r) -> p a r l", l=P, r=2),
                                     stage[:, c % NSTAGE, :].rearrange("p (a r l) -> p a r l", l=P, r=2),
                                     ACT.Copy).then_inc(byte_ready, 1)
                if not (isinstance(s, int) and s == 0):
                    for part in row_parts("act", octets, c):
                        rows(s, part, octets_before(s, first, octets))

        superblocks(act, body)
        for part in row_order("act"):
            rows(SB, part, sum(EARLY))
        act.wait_ge(biased, SB)
        act.dma_start(y_dram[:, SB - 1], yb[:, :, :]).then_inc(y_stored, 16)

        for s in range(SB):
            act.wait_ge(l1_octet, octets_through_late(s))
            if s >= 2:
                act.wait_ge(tail_out, s - 1)
            nc.scalar.activation(tail_part(s).rearrange("p (a b) f -> p a b f", b=2),
                                 tail_ps(s).rearrange("p a (b f) -> p a b f", b=2)[:, :, :, D:2 * D],
                                 ACT.Copy).then_inc(tail_low, 1)

    @block.tensor
    def _(pe):
        pe.wait_ge(weights_in, 96)
        nc.tensor.matmul(ps1[:, 0, 0:1], waT[0:2, :], a2[0:2, :], start=True, stop=True).then_inc(g_mm, 1)
        pe.wait_ge(g_cp, 1)
        nc.tensor.matmul(ps1[:, 0, 1:2], wTt, wa2, start=True, stop=True).then_inc(g_mm, 1)
        pe.wait_ge(wsq_done, 2)
        pe.wait_ge(vec_consts, 3)
        nc.tensor.matmul(ps1[:, 1, 0:2 * D], ones, wsq, start=True, stop=True).then_inc(g_mm, 1)
        pe.wait_ge(pool_consts, 2)
        pe.wait_ge(g_cp, 2)
        for g in range(17):
            if g < 16:
                pe.wait_ge(centred, g // 4 + 1)
                if g >= 2:
                    pe.wait_ge(hT_done, g - 1)
                for b in range(4):
                    last = nc.tensor.transpose(setT[g % 2][:, b * P:(b + 1) * P], X[:, 4 * g + b, :], ident[:, :])
                last.then_inc(tr_done, 1)
            if g:
                k = g - 1
                pe.wait_ge(hT_done, k + 1)
                if k >= 2:
                    pe.wait_ge(*((hp_cp, k - 1) if k < 10 else (hp_cp2, k - 9)))
                for b in range(4):
                    last = nc.tensor.matmul(setH[k % 2][:, b // 2, (b % 2) * (D + 1):(b % 2 + 1) * (D + 1)],
                                            hT[k % 2][:, b * P:(b + 1) * P], wG, start=(b % 2 == 0), stop=(b % 2 == 1),
                                            skip_group_check=True)
                last.then_inc(hp_mm, 1)
        pe.wait_ge(rstd_done, 1)
        pe.wait_ge(hp_cp2, 8)
        for t in range(T):
            last = nc.tensor.matmul(ps1[:, 0, 128:256], rstd[:, t:t + 1].broadcast_to([P, P]), H[:, t, :],
                                    start=(t == 0), stop=(t == T - 1))
            if t in (7, T - 1):
                last.then_inc(mean_mm, 1)
        pe.wait_ge(v0_cols, 1)

        def chunk(s, c):
            n = CH * s + c
            pe.wait_ge(mask_ready, n + 1)
            for t in range(CT):
                k = CT * c + t
                for b in range(BL):
                    last = nc.tensor.matmul(ps0[:, b, 0:NV0], mask[:, c % NMASK, t * IW + b * P:t * IW + (b + 1) * P],
                                            V0[:, k, :], start=(k == 0), stop=(k == T - 1))
            last.then_inc(l0_done, 1)

        def octet(sums, count, o, slot, begin, end):
            pe.wait_ge(unpacked, count + 1)
            for t in range(OCT):
                for b in range(BL):
                    last = nc.tensor.matmul(sums[:, b // 2, (b % 2) * 2 * D:(b % 2 + 1) * 2 * D],
                                            unp[:, slot, b % 2, t * 256 + (b // 2) * P:t * 256 + (b // 2 + 1) * P],
                                            V1[:, OCT * o + t, :], start=(begin and t == 0 and b % 2 == 0),
                                            stop=(end and t == OCT - 1), skip_group_check=True)
            return last

        def rows(s, part):
            e = s - 1
            if part == "turn":
                pe.wait_ge(h_ready, e + 1)
                for b in range(BL):
                    last = nc.tensor.transpose(psT[:, b * P:(b + 1) * P], num[:, b, :], ident[:, :])
                last.then_inc(rowT_done, 1)
            if part == "weigh":
                pe.wait_ge(rowT_copied, e + 1)
                wait(pe, v_ready, e)
                for b in range(BL):
                    last = nc.tensor.matmul(psH[:, b * P:(b + 1) * P], ev[:, b, 0:D], WT[:, :],
                                            start=(b == 0), stop=(b == BL - 1), skip_group_check=True)
                last.then_inc(rowW_done, 1)

        def body(s, first, octets):
            for c in range(CH):
                if c == 0:
                    take(s, first, octets, -1)
                    if isinstance(s, int) and s == 0:
                        pe.wait_ge(v0_lo, 1)
                    else:
                        pe.wait_ge(ev_ready, s)
                if isinstance(s, int) and s == 0 and c % 4 == 0 and c:
                    pe.wait_ge(v0_lo, c // 4 + 1)
                chunk(s, c)
                if not (isinstance(s, int) and s == 0):
                    for part in row_parts("pe", octets, c):
                        rows(s, part)
                take(s, first, octets, c)

        def take(s, first, octets, c):
            for o, at in enumerate(PLACES[octets]):
                if at == c:
                    if isinstance(s, int) and s - 2 < FIRST_L1:
                        pe.wait_ge(mean_cp, 1)
                    elif o == 0:
                        pe.wait_ge(l1_sum, s - 2)
                    pe.wait_ge(v1_ready, 2 * o + 2)
                    octet(ps1, octets_before(s, first, octets) + o, o, o % 2, o == 0, o == octets - 1).then_inc(l1_octet, 1)

        superblocks(pe, body)

        for count, (s, o) in enumerate(LATE_OCTETS, sum(EARLY)):
            if o == EARLY[s]:
                wait(pe, tail_sum, s - 1)
                if s == 0:
                    pe.wait_ge(ev_ready, SB)
                for b in range(BL):
                    if s == SB - 1:
                        pe.wait_ge(v1_ready, SB)
                    nc.tensor.matmul(tail_ps(s)[:, b // 2, (b % 2) * 2 * D:(b % 2 + 1) * 2 * D], ident2[:, :],
                                     V1[:, BL * s + b, :], start=(b % 2 == 0), stop=False, skip_group_check=True)
            if (s, o) == (0, SB // 2 - 1):
                pe.wait_ge(v1_ready, SB)
            octet(tail_ps(s), count, o, count % 2, False, o == SB // 2 - 1).then_inc(l1_octet, 1)
            for part in {(0, 3): ["turn"], (0, 5): ["weigh"]}.get((s, o), ()):
                rows(SB, part)

    @block.vector
    def _(dve):
        steps = [0]

        def link(ins):
            steps[0] += 1
            ins.then_inc(vec_step, 1)
            dve.wait_ge(vec_step, steps[0])

        nc.vector.memset(ones, 1.0).then_inc(vec_consts, 1)
        nc.vector.memset(epsc, EPS).then_inc(vec_consts, 1)
        dve.wait_ge(pool_consts, 2)
        nc.vector.tensor_scalar(ident2[:, :], ident[:, :], 2.0, None, ALU.mult).then_inc(vec_consts, 1)

        def stats(q):
            dve.wait_ge(x_part[q], 16)
            for t in range(16 * q, 16 * q + 16):
                last = nc.vector.bn_stats(st[:, t, :], X[:, t, :])
            link(last)
            for t in range(16 * q, 16 * q + 16):
                last = nc.vector.bn_aggr(mv[:, t, :], st[:, t, :])
            last.then_inc(var_done, 1)

        stats(0)
        dve.wait_ge(weights_in, 96)
        nc.vector.tensor_tensor(wsq[:, 0:D], wG[:, 0:D], wG[:, 0:D], ALU.mult).then_inc(wsq_done, 1)
        nc.vector.tensor_tensor(wsq[:, D:2 * D], WT[:, :], WT[:, :], ALU.mult).then_inc(wsq_done, 1)
        dve.wait_ge(g_mm, 1)
        nc.vector.tensor_copy(wa2, ps1[:, 0, 0:1]).then_inc(g_cp, 1)
        dve.wait_ge(g_mm, 2)
        nc.vector.tensor_copy(wG[:, D:D + 1], ps1[:, 0, 1:2]).then_inc(g_cp, 1)
        stats(1)
        dve.wait_ge(g_mm, 3)
        for k in range(2):
            link(nc.vector.tensor_reduce(cmax[:, k:k + 1], ps1[:, 1, k * D:(k + 1) * D], AX.X, ALU.max))
        nc.vector.tensor_scalar(cmax, cmax, 1e-30, None, ALU.max).then_inc(norms_done, 1)
        stats(2)
        stats(3)
        for g in range(8, 16):
            dve.wait_ge(hp_mm, g + 1)
            copy_products(nc.vector.tensor_copy, g)
        dve.wait_ge(std_done, 1)
        nc.vector.reciprocal(rstd, sd).then_inc(rstd_done, 1)
        dve.wait_ge(norm_sqrt, 1)
        link(nc.vector.reciprocal(sig[:, 6:8], cmax))
        link(nc.vector.tensor_scalar(sig[:, 6:8], sig[:, 6:8], BOUND, None, ALU.mult))
        link(nc.vector.tensor_scalar(sig[:, 0:2].bitcast(U32), sig[:, 6:8].bitcast(U32), 0x7F800000, None,
                                     ALU.bitwise_and))
        link(nc.vector.tensor_scalar(sig[:, 2:3], sig[:, 0:1], 1.0 / M_SCALE, None, ALU.mult))
        link(nc.vector.reciprocal(sig[:, 3:4], sig[:, 1:2]))
        link(nc.vector.tensor_scalar(sig[:, 4:5], sig[:, 3:4], 0.5, None, ALU.mult))
        dve.wait_ge(rstd_done, 1)
        dve.wait_ge(hp_cp, 8)
        dve.wait_ge(hp_cp2, 8)
        link(nc.vector.tensor_tensor(f, f, rstd, ALU.mult))
        link(nc.vector.tensor_scalar(kf, f, LOG2E, ROUND, ALU.mult, ALU.add))
        link(nc.vector.tensor_scalar(kf, kf, -ROUND, None, ALU.add))
        nc.vector.tensor_reduce(kmax, kf, AX.X, ALU.max).then_inc(kmax_done, 1)
        link(nc.vector.scalar_tensor_tensor(r1, kf, -LN2_HI, f, ALU.mult, ALU.add))
        nc.vector.scalar_tensor_tensor(r1, kf, -LN2_LO, r1, ALU.mult, ALU.add).then_inc(frac_done, 1)
        dve.wait_ge(exp_done, 1)
        link(nc.vector.scalar_tensor_tensor(mS, m, sig[:, 0:1], rstd, ALU.mult, ALU.mult))

        def scaled_products(q):
            sl = slice(16 * q, 16 * q + 16)
            nc.vector.tensor_tensor(X[:, sl, :], H[:, sl, :], wide(mS[:, sl]), ALU.mult).then_inc(v0_f32, 1)

        scaled_products(0)
        link(nc.vector.tensor_scalar(m, m, M_SCALE, None, ALU.mult))
        link(nc.vector.tensor_copy(V0[:, :, 2 * D], m))
        nc.vector.tensor_tensor(V0[:, :, 2 * D + 1], m, V0[:, :, 2 * D], ALU.subtract)
        dve.wait_ge(kall_done, 1)
        link(nc.vector.tensor_scalar(ke, kf, kall, float(TOP), ALU.subtract, ALU.add))
        link(nc.vector.tensor_scalar(ke, ke, float(LOW), None, ALU.max))
        link(nc.vector.tensor_scalar(sbit, ke, 127.0, float(2 ** 23), ALU.add, ALU.mult))
        link(nc.vector.tensor_copy(scale2[:, :].bitcast(I32), sbit))
        for b in range(BUCKETS):
            last = nc.vector.tensor_scalar(w15[b], ke, -1.0, float(TOP - 14 - 30 * b + 15), ALU.mult, ALU.add)
        link(last)
        for b in range(BUCKETS):
            last = nc.vector.scalar_tensor_tensor(q1[b], w15[b], 1.0, w15[b], ALU.is_ge, ALU.mult)
        link(last)
        for b in range(BUCKETS):
            last = nc.vector.scalar_tensor_tensor(q2[b], w15[b], 30.0, q1[b], ALU.is_le, ALU.mult)
        link(last)
        for b in range(BUCKETS):
            last = nc.vector.tensor_scalar(V0[:, :, 2 * D + 2 + b].bitcast(U16), q2[b], 1024.0, None, ALU.mult)
        last.then_inc(v0_cols, 1)
        def pack(s, c):
            if c < 2:
                return
            dve.wait_ge(byte_ready, CH * s + c + 1)
            if c >= 4:
                dve.wait_ge(packed, 14 * s + (c - 2) - 1)
            dst = bits[:, s, (c % 2) * CT * IW:(c % 2 + 1) * CT * IW].bitcast(U32)
            nc.vector.scalar_tensor_tensor(dst, byte[:, c % 2, :].bitcast(U32), c // 2, dst,
                                           ALU.logical_shift_left, ALU.bitwise_or).then_inc(packed, 1)

        def unpack(s, o, slot, free):
            wait(dve, l1_octet, free)
            for par in range(2):
                shift = 14 - o - 8 * par
                last = nc.vector.tensor_scalar(
                    unp[:, slot, par, :].bitcast(U32), bits[:, s, :].bitcast(U32), abs(shift), 0x40004000,
                    ALU.logical_shift_left if shift >= 0 else ALU.logical_shift_right, ALU.bitwise_and)
            last.then_inc(unpacked, 1)

        def rows(s, part):
            e = s - 1

            def step(ins, k):
                ins.then_inc(row_step, 1)
                dve.wait_ge(row_step, ROW_STEPS * e + k)

            if part == "sums":
                dve.wait_ge(ev_ready, e + 1)
                wait(dve, v1_ready, e)
                nc.vector.tensor_tensor(cprod[:, :, :], ev[:, :, 2 * D + 2:NV0],
                                        cw[:, :].unsqueeze(1).broadcast_to([P, BL, BUCKETS]), ALU.mult)
                step(nc.vector.tensor_tensor(den[:, :], ev[:, :, 2 * D], ev[:, :, 2 * D + 1], ALU.add), 1)
                step(nc.vector.tensor_reduce(cnt[:, :], cprod[:, :, :], AX.X, ALU.add), 2)
                nc.vector.tensor_tensor(num[:, :, :], ev[:, :, 0:D], ev[:, :, D:2 * D], ALU.add)
                step(nc.vector.tensor_scalar(zero_row[:, :], cnt[:, :], 0.0, None, ALU.is_equal), 3)
                nc.vector.scalar_tensor_tensor(den[:, :], den[:, :], sig[:, 2:3], zero_row[:, :], ALU.mult,
                                               ALU.add).then_inc(z_ready, 1)
                dve.wait_ge(z_ready, e + 1)
                step(nc.vector.reciprocal(rden[:, :], den[:, :]), 4)
                step(nc.vector.tensor_tensor(num[:, :, :], num[:, :, :], wide(rden[:, :]), ALU.mult), 5)
            if part == "stats":
                dve.wait_ge(xz_ready, e + 1)
                nc.vector.scalar_tensor_tensor(xb[:, :, :], num[:, :, :], 0.0, xb[:, :, :], ALU.max,
                                               ALU.add).then_inc(x1_ready, 1)
                dve.wait_ge(x1_ready, e + 1)
                for b in range(BL):
                    last = nc.vector.bn_stats(bst[:, b, :], xb[:, b, :])
                last.then_inc(rstat_done, 1)
                dve.wait_ge(rstat_done, 2 * e + 1)
                nc.vector.tensor_scalar(sq[:, BL:2 * BL], cnt[:, :], 1.0, None, ALU.add)
                for b in range(BL):
                    last = nc.vector.bn_aggr(bmv[:, b, :], bst[:, b, :])
                last.then_inc(rstat_done, 1)
                dve.wait_ge(rstat_done, 2 * e + 2)
                nc.vector.tensor_scalar(sq[:, 0:BL], bmv[:, :, 1], EPS, None, ALU.add).then_inc(sq_ready, 1)
            if part == "scales":
                if not (isinstance(s, int) and s - 2 < FIRST_L1):
                    dve.wait_ge(y_ready, s - 2)
                dve.wait_ge(sqrt_done, e + 1)
                nc.vector.reciprocal(rs[:, :], rs[:, :]).then_inc(rs_recip, 1)
                dve.wait_ge(rs_recip, e + 1)
                nc.vector.scalar_tensor_tensor(nbias[:, :], bmv[:, :, 0], -1.0, rs[:, 0:BL], ALU.mult, ALU.mult)
                nc.vector.tensor_copy(dalls[:, e, :], rs[:, BL:2 * BL])
                nc.vector.tensor_scalar(dsig[:, :], rs[:, BL:2 * BL], sig[:, 1:2], None, ALU.mult)
                nc.vector.tensor_scalar(dback[:, :], rs[:, BL:2 * BL], sig[:, 4:5], None,
                                        ALU.mult).then_inc(rs_ready, 1)
            if part == "low" and not (isinstance(s, int) and s - 2 < FIRST_L1):
                dve.wait_ge(l1_low, s - 2)
                part4 = low[:, :, :].rearrange("p (a b) f -> p a b f", b=2)
                nc.vector.tensor_tensor(part4, ps1[:, :, :].rearrange("p a (b f) -> p a b f", b=2)[:, :, :, 0:D],
                                        part4, ALU.add).then_inc(l1_sum, 1)
            if part == "v":
                dve.wait_ge(rowW_done, e + 1)
                dve.wait_ge(rs_ready, e + 1)
                nc.vector.tensor_tensor(num[:, :, :], psH[:, :].rearrange("p (b f) -> p b f", b=BL),
                                        wide(dsig[:, :]), ALU.mult).then_inc(v_ready, 1)

        def body(s, first, octets):
            place = {}
            for o, at in enumerate(PLACES[octets]):
                place[at + 1 if at in place else at] = o

            def take(c):
                if c in place:
                    o = place[c]
                    if o == 0:
                        dve.wait_ge(packed, 14 * s)
                    unpack(s - 1, o, o % 2, octets_before(s, first, octets) + (o - 1 if o >= 2 else 0))

            take(-1)
            for c in range(CH):
                n = CH * s + c
                dve.wait_ge(adj_landed[c % NSTAGE], 4 * 16 * s + 16 * (c // NSTAGE + 1))
                wait(dve, l0_done, n - NMASK + 1)
                for t in range(CT):
                    k = CT * c + t
                    last = nc.vector.tensor_scalar(mask[:, c % NMASK, t * IW:(t + 1) * IW],
                                                   stage[:, c % NSTAGE, t * IW:(t + 1) * IW], 0.0,
                                                   scale2[:, k:k + 1], ALU.is_gt, ALU.mult)
                last.then_inc(mask_ready, 1)
                if isinstance(s, int) and s == 0:
                    if c < 3:
                        scaled_products(c + 1)
                    if c == 3:
                        dve.wait_ge(mean_mm, 2)
                        nc.vector.tensor_scalar(meanh[:, :], ps1[:, 0, 128:256], 1.0 / N, 0.0, ALU.mult,
                                                ALU.max).then_inc(mean_cp, 1)
                pack(s, c)
                if not (isinstance(s, int) and s == 0):
                    for part in row_parts("dve", octets, c):
                        rows(s, part)
                take(c)

        superblocks(dve, body)

        def finish(s):
            ybuf = [xb, num][s % 2]
            part = tail_part(s)
            part4 = part.rearrange("p (a b) f -> p a b f", b=2)
            dve.wait_ge(tail_low, s + 1)
            nc.vector.tensor_tensor(part4, tail_ps(s).rearrange("p a (b f) -> p a b f", b=2)[:, :, :, 0:D], part4,
                                    ALU.add).then_inc(tail_sum, 1)
            dve.wait_ge(tail_sum, s + 1)
            dve.wait_ge(dall_done, 1)
            nc.vector.tensor_tensor(part, part, wide(dalls[:, s, :]), ALU.mult).then_inc(tail_scaled, 1)
            dve.wait_ge(tail_scaled, s + 1)
            dve.wait_ge(tail_x[s % 2], 16 * (s // 2 + 1))
            nc.vector.tensor_tensor(ybuf[:, :, :], ybuf[:, :, :], part, ALU.add).then_inc(tail_out, 1)

        dve.wait_ge(packed, 14 * SB)
        for count, (s, o) in enumerate(LATE_OCTETS, sum(EARLY)):
            unpack(s, o, count % 2, max(sum(EARLY), count - 1))
            if s == 0:
                for part in {1: ["low", "sums"], 2: ["stats"], 3: ["scales"], 6: ["v"]}.get(o, ()):
                    rows(SB, part)
            elif o == EARLY[s]:
                if s == 1:
                    nc.vector.tensor_scalar(dall[:, :], dall[:, :], sig[:, 4:5], None, ALU.mult).then_inc(dall_done, 1)
                finish(s - 1)
        finish(SB - 1)

    ctx.close()


_INS = [("adj", (SB, CH, P, CT * IW)), ("x", (P, SB, BL, D)), ("w", (D, D)), ("wT", (D, D)), ("waT", (2, D)),
        ("a", (2, 1)), ("WT", (D, D)), ("b", (P, D))]


def kernel(x, adj, L0_gnn_w, L0_gnn_w_a, L0_gnn_a, L1_gnn_W, L1_gnn_b):
    import concourse.bacc as bacc
    from concourse.bass_utils import run_bass_kernel_spmd

    x, adj, w, w_a, a, W, b = (np.asarray(v) for v in (x, adj, L0_gnn_w, L0_gnn_w_a, L0_gnn_a, L1_gnn_W, L1_gnn_b))
    chunks = adj.reshape(SB, IW, CH, CT, P).transpose(0, 2, 4, 3, 1).reshape(SB, CH, P, CT * IW)
    arrays = {
        "adj": np.ascontiguousarray(chunks),
        "x": np.ascontiguousarray(x.reshape(T, P, D).transpose(1, 0, 2)).reshape(P, SB, BL, D),
        "w": np.ascontiguousarray(w),
        "wT": np.ascontiguousarray(w.T),
        "waT": np.ascontiguousarray(w_a.T),
        "a": np.ascontiguousarray(a[2:4]),
        "WT": np.ascontiguousarray(W.T),
        "b": np.ascontiguousarray(np.broadcast_to(b[None, :], (P, D))),
    }
    nc = bacc.Bacc("TRN2", target_bir_lowering=False, num_devices=1, dynamic_dma_scratch_size=1024)
    ins = [nc.dram_tensor(f"{name}_in", shape, F32, kind="ExternalInput").ap() for name, shape in _INS]
    out = nc.dram_tensor("out", (P, SB, BL, D), F32, kind="ExternalOutput").ap()
    build(nc, ins, out)
    r = run_bass_kernel_spmd(nc, [{f"{k}_in": v for k, v in arrays.items()}], core_ids=[0])
    got = r.results[0]["out"]
    return np.ascontiguousarray(got.reshape(P, T, D).transpose(1, 0, 2)).reshape(N, D)
```

```python
from contextlib import ExitStack
import math

import numpy as np
import concourse.bass as bass
from concourse import mybir

F32, F16, BF16 = mybir.dt.float32, mybir.dt.float16, mybir.dt.bfloat16
U8, U16, U32, I32 = mybir.dt.uint8, mybir.dt.uint16, mybir.dt.uint32, mybir.dt.int32
ALU = mybir.AluOpType
ACT = mybir.ActivationFunctionType
AX = mybir.AxisListType

P = 128
N = 8192
D = 128
T = N // P
BL = 4
SB = T // BL
IW = BL * P
CT = 4
CH = T // CT
OCT = 8
NSTAGE = 4
NMASK = 4
ACT_MASKS = range(1, CH, 2)
QUARTERS_SCALED = {2: 1, 3: 2, 7: 3}
QUARTERS_ROUNDED = {3: 1, 4: 2, 8: 3}
EPS = 1e-5

LOG2E = float(np.float32(1.0 / math.log(2.0)))
LN2_HI = float(np.float32(0.693359375))
LN2_LO = float(np.float32(math.log(2.0) - 0.693359375))
ROUND = float(3 << 22)
TOP = 60
BUCKETS = 3
LOW = TOP - 30 * BUCKETS + 1
M_SCALE = 1024.0
SPREAD = (30 * BUCKETS - 1) * math.log(2.0) - 1.5
NV0 = 2 * D + 2 + BUCKETS
BOUND = 2.0 ** 14 / (math.sqrt(D) * 1.42)

FIRST_L1 = 2
GROUPS = [(0, 1, 0), (1, 1, 0), (2, 1, 0), (3, 1, 1)] + [(2 * p, 2, p) for p in range(2, SB // 2)]
PLACES = {0: [], 1: [13], 2: [-1, 13], 3: [-1, 5, 13], 4: [-1, 3, 7, 13], 5: [-1, 3, 7, 10, 13],
          6: [-1, 2, 4, 7, 10, 13], 7: [-1, 2, 4, 6, 8, 11, 13]}
BACKLOG = {3: (6, [(8, 0), (11, 1)])}
BACKLOG_ROWS = [0, 1]
FIRST_BACKLOG = 6
ROW_STEPS = 5


def sequence(octets):
    back, extra = BACKLOG.get(octets, (0, []))
    return sorted([(at, 0, o) for o, at in enumerate(PLACES[octets])] + [(at, back, o) for at, o in extra])


def taken_by(e):
    taken = []
    for first, count, octets in GROUPS:
        for s in range(first, first + count):
            for _, back, o in sequence(octets):
                if (s - back if back else s - 1) == e:
                    taken.append(o)
    return taken


ROW_PLACES = {
    "act": [dict(evac=0, low=1, sqrt=2, relu=3, store=4, turn=6, high=9),
            dict(evac=2, low=0, sqrt=4, relu=5, store=6, turn=8, high=12)],
    "dve": [dict(low=1, sums=1, stats=2, scales=3, v=9), dict(low=0, sums=2, stats=3, scales=4, v=11)],
    "pe": [dict(turn=5, weigh=7), dict(turn=5, weigh=7)],
}


LATE = 2


def row_parts(engine, octets, c):
    return [k for k, at in ROW_PLACES[engine][octets >= LATE].items() if at == c]


LATE_OF = [[o for o in range(SB // 2) if o not in taken_by(s)] for s in range(SB)]
LATE_OCTETS = [(s, o) for s in range(SB) for o in LATE_OF[s]]
LATE_OCTETS.insert(len(LATE_OF[0]) + 1, LATE_OCTETS.pop(len(LATE_OF[0]) - 1))
LAST_OF = [LATE_OCTETS.index((s, LATE_OF[s][-1])) for s in range(SB)]
EARLY_OCTETS = SB * SB // 2 - len(LATE_OCTETS)


def row_order(engine):
    return sorted(ROW_PLACES[engine][0], key=ROW_PLACES[engine][0].get)


def act_masks_through(s, c):
    return len(ACT_MASKS) * (s - 1) + sum(k <= c for k in ACT_MASKS)


def octets_before(s, first, octets):
    before = sum(count * len(sequence(k)) for start, count, k in GROUPS if start < first)
    return before + (s - first) * len(sequence(octets))


def shares(s):
    return s - 1 - FIRST_L1


def octets_through_late(s):
    return EARLY_OCTETS + LAST_OF[s] + 1


def build(nc, ins, outs):
    adj, x_in, w_in, wT_in, waT_in, a_in, WT_in, b_in = ins
    out = outs
    att_dram = nc.dram_tensor("att_scratch", (P, SB, BL, D), F32, kind="Internal").ap()
    y_dram = nc.dram_tensor("y_scratch", (P, SB, BL, D), F32, kind="Internal").ap()
    backlog_dram = nc.dram_tensor("backlog_scratch", (P, len(BACKLOG_ROWS), BL, D), F32, kind="Internal").ap()
    ctx = ExitStack()

    def sb(name, shape, dt):
        return ctx.enter_context(nc.sbuf_tensor(name, shape, dt))

    def sem(name):
        return ctx.enter_context(nc.semaphore(name))

    bits = sb("bits", [P, SB, OCT * IW], U8)
    V0 = sb("V0", [P, T, NV0], F16)
    V1 = sb("V1", [P, T, 2 * D], F16)
    stage = sb("stage", [P, NSTAGE, CT * IW], F32)
    mask = sb("mask", [P, NMASK, CT * IW], BF16)
    byte = sb("byte", [P, 2, CT * IW], U8)
    unp = sb("unp", [P, 2, 2, OCT * IW // 2], F16)
    ev = sb("ev", [P, BL, NV0], F32)
    num = sb("num", [P, BL, D], F32)
    xb = sb("xb", [P, BL, D], F32)
    yb = sb("yb", [P, BL, D], F32)
    low = sb("low", [P, BL, D], F32)
    ident = sb("ident", [P, P], F32)
    WT = sb("WT", [P, D], F32)
    bias = sb("bias", [P, D], F32)
    meanh = sb("meanh", [P, D], F32)
    scale2 = sb("scale2", [P, T], F32)
    dall = sb("dall", [P, T], F32)
    sig = sb("sig", [P, 8], F32)
    cw = sb("cw", [P, BUCKETS], F32)
    den = sb("den", [P, BL], F32)
    cprod = sb("cprod", [P, BL, BUCKETS], F32)
    zero_row = sb("zero_row", [P, BL], F32)
    cnt = sb("cnt", [P, BL], F32)
    rden = sb("rden", [P, BL], F32)
    bst = sb("bst", [P, BL, 6], F32)
    bmv = sb("bmv", [P, BL, 2], F32)
    sq = sb("sq", [P, 2 * BL], F32)
    rs = sb("rs", [P, 2 * BL], F32)
    nbias = sb("nbias", [P, BL], F32)
    dsig = sb("dsig", [P, BL], F32)
    dback = sb("dback", [P, BL], F32)
    dself = sb("dself", [P, BL], F32)
    own = sb("own", [P, BL, D], F32)
    wide_f = sb("wide_f", [P, 1], I32)
    attg = sb("attg", [P, BL, D], F32)
    one = sb("one", [P, 1], F32)

    low_half = bits[:, 0:SB // 2, :].rearrange("p s n -> p (s n)").bitcast(F32)
    high_half = bits[:, SB // 2:SB, :].rearrange("p s n -> p (s n)").bitcast(F32)
    H = low_half.rearrange("p (t f) -> p t f", f=D)
    X = high_half.rearrange("p (t f) -> p t f", f=D)
    v1f = V1[:, :, :].rearrange("p t f -> p (t f)").bitcast(F32)
    hT = [v1f[:, 512 * k:512 * k + 512] for k in range(2)]
    at = [1024]

    def small(n):
        a = at[0]
        at[0] += n
        return v1f[:, a:a + n]

    ones = small(P)
    wG = small(D + 1)
    wTt = small(D)
    waT = small(D)
    a2 = small(1)
    wa2 = small(1)
    wsq = small(2 * D)
    cmax = small(2)
    st = small(T * 6).rearrange("p (t k) -> p t k", k=6)
    mv = small(T * 2).rearrange("p (t k) -> p t k", k=2)
    sd = small(T)
    rstd = small(T)
    epsc = small(1)
    f = small(T)
    kf = small(T)
    r1 = small(T)
    m = small(T)
    mS = small(T)
    ext = small(2)
    ext_all = small(2)
    kall = ext_all[:, 0:1]
    spread = small(1)
    ke = small(T)
    sbit = small(T).bitcast(I32)
    w15 = [small(T) for _ in range(BUCKETS)]
    q1 = [small(T) for _ in range(BUCKETS)]
    q2 = [small(T) for _ in range(BUCKETS)]

    fs = small(T)
    nf1 = small(1)
    unpF = unp[:, :, :, :].rearrange("p a b n -> p (a b n)").bitcast(F32)
    maskF = mask[:, :, :].rearrange("p a n -> p (a n)").bitcast(F32)
    g_adj = unpF[:, 0:CT * IW]
    g_max, g_shift, g_exp, g_prob = [unpF[:, CT * IW + k * IW:CT * IW + (k + 1) * IW] for k in range(4)]
    g_diag, g_tmp = maskF[:, 0:IW], maskF[:, IW:2 * IW]
    g_h = maskF[:, 2 * IW:2 * IW + D + 1]
    g_col, g_den = maskF[:, 1200:1200 + BL], maskF[:, 1216:1216 + BL]
    g_zero = maskF[:, 1232:1232 + BL]

    ps0 = ctx.enter_context(nc.psum_tensor("ps0", [P, BL, 512], F32))
    ps1 = ctx.enter_context(nc.psum_tensor("ps1", [P, 2, 512], F32))
    psT = ctx.enter_context(nc.psum_tensor("psT", [P, 512], F32))
    psH = ctx.enter_context(nc.psum_tensor("psH", [P, 512], F32))
    setT = [psT, psH]
    setH = [ps0[:, 0:2, :], ps0[:, 2:4, :]]

    weights_in = sem("weights_in")
    x_part = [sem(f"x_part{q}") for q in range(4)]
    pool_consts = sem("pool_consts")
    vec_consts = sem("vec_consts")
    std_done = sem("std_done")
    w_mm = sem("w_mm")
    g_cp = sem("g_cp")
    tr_done = sem("tr_done")
    hT_done = sem("hT_done")
    hp_mm = sem("hp_mm")
    hp_cp = sem("hp_cp")
    hp_cp2 = sem("hp_cp2")
    centred = sem("centred")
    norm_sqrt = sem("norm_sqrt")
    mean_mm = sem("mean_mm")
    mean_cp = sem("mean_cp")
    rstd_done = sem("rstd_done")
    var_done = sem("var_done")
    norms_done = sem("norms_done")
    wsq_done = sem("wsq_done")
    frac_done = sem("frac_done")
    kmax_done = sem("kmax_done")
    v0_cols = sem("v0_cols")
    vec_step = sem("vec_step")
    exp_done = sem("exp_done")
    kall_done = sem("kall_done")
    scale_known = sem("scale_known")
    v0_f32 = sem("v0_f32")
    v0_hi = sem("v0_hi")
    v0_lo = sem("v0_lo")
    wide_known = sem("wide_known")
    g_free = sem("g_free")
    g_landed = sem("g_landed")
    g_vec = sem("g_vec")
    g_maxed = sem("g_maxed")
    g_turned = sem("g_turned")
    g_diag_ready = sem("g_diag_ready")
    g_spread = sem("g_spread")
    g_arg = sem("g_arg")
    g_exped = sem("g_exped")
    g_ready = sem("g_ready")
    g_mm = sem("g_mm_rows")
    g_att = sem("g_att")
    g_stored = sem("g_stored")
    att_loaded = sem("att_loaded")
    att_used = sem("att_used")
    adj_landed = [sem(f"adj_landed{k}") for k in range(NSTAGE)]
    mask_ready = sem("mask_ready")
    act_mask_ready = sem("act_mask_ready")
    byte_ready = sem("byte_ready")
    packed = sem("packed")
    l0_done = sem("l0_done")
    unpacked = sem("unpacked")
    l1_octet = sem("l1_octet")
    x_loaded = sem("x_loaded")
    ev_ready = sem("ev_ready")
    row_step = sem("row_step")
    z_ready = sem("z_ready")
    xz_ready = sem("xz_ready")
    x1_ready = sem("x1_ready")
    sq_ready = sem("sq_ready")
    sqrt_done = sem("sqrt_done")
    rs_ready = sem("rs_ready")
    h_ready = sem("h_ready")
    rowT_done = sem("rowT_done")
    rowT_copied = sem("rowT_copied")
    rowW_done = sem("rowW_done")
    v_ready = sem("v_ready")
    v1_hi = sem("v1_hi")
    v1_ready = sem("v1_ready")
    l1_low = sem("l1_low")
    l1_scaled = sem("l1_scaled")
    biased = sem("biased")
    own_ready = sem("own_ready")
    own_added = sem("own_added")
    zrow_done = sem("zrow_done")
    rstat_done = sem("rstat_done")
    rs_recip = sem("rs_recip")
    dall_done = sem("dall_done")
    l1_sum = sem("l1_sum")
    y_ready = sem("y_ready")
    y_stored = sem("y_stored")
    tail_x = [sem(f"tail_x{k}") for k in range(2)]
    tail_low = sem("tail_low")
    backlog_copied = sem("backlog_copied")
    backlog_stored = sem("backlog_stored")
    backlog_loaded = sem("backlog_loaded")
    backlog_added = sem("backlog_added")
    tail_sum = sem("tail_sum")
    tail_scaled = sem("tail_scaled")
    tail_out = sem("tail_out")
    out_stored = [sem(f"out_stored{k}") for k in range(2)]

    def wait(eng, s, value):
        if not isinstance(value, int) or value > 0:
            eng.wait_ge(s, value)

    def superblocks(eng, body):
        for first, count, octets in GROUPS:
            if count == 1:
                body(first, first, octets)
            else:
                with eng.Fori(first, first + count) as s:
                    body(s, first, octets)

    def wide(v):
        return v.unsqueeze(2).broadcast_to([P, v.shape[1], D])

    def per_block(v):
        return v.unsqueeze(1).broadcast_to([P, BL, D])

    def tail_ps(s):
        return ps0[:, 2 * (s % 2):2 * (s % 2) + 2, :]

    def backlog_sums(k):
        return stage[:, k // BL, k % BL * IW:(k % BL + 1) * IW].rearrange("p (b f) -> p b f", b=BL)

    def tail_part(s):
        return ev[:, :, D * (s % 2):D * (s % 2) + D]

    def copy_products(copy, g):
        src = setH[g % 2][:, :, 0:2 * (D + 1)].rearrange("p a (b f) -> p a b f", b=2)
        copy(H[:, 4 * g:4 * g + 4, :].rearrange("p (a b) f -> p a b f", b=2), src[:, :, :, 0:D])
        copy(f[:, 4 * g:4 * g + 4].rearrange("p (a b) -> p a b", b=2), src[:, :, :, D]).then_inc(
            hp_cp if g < 8 else hp_cp2, 1)

    V1s = V1[:, :, :].rearrange("p (s b) f -> p s b f", b=BL)
    dalls = dall[:, :].rearrange("p (s b) -> p s b", b=BL)

    block = ctx.enter_context(nc.Block())

    @block.sync
    def _(sp):
        for q in range(4):
            sp.dma_start(X[:, 16 * q:16 * q + 16, :],
                         x_in[:, 4 * q:4 * q + 4].rearrange("p s b f -> p (s b) f")).then_inc(x_part[q], 16)
            if q == 0:
                for dst, src in [(wG[:, 0:D], w_in), (wTt, wT_in), (waT[0:2, :], waT_in), (a2[0:2, :], a_in),
                                 (WT[:, :], WT_in), (bias[:, :], b_in)]:
                    sp.dma_start(dst, src).then_inc(weights_in, 16)

        for c in range(NSTAGE):
            sp.dma_start(stage[:, c, :], adj[0, c]).then_inc(adj_landed[c], 16)
        sp.wait_ge(wide_known, 1)
        wide_sp = sp.value_load(wide_f[0:1, 0:1], min_val=0, max_val=1)
        with sp.If(wide_sp > 0):
            with sp.Fori(0, SB) as s:
                for sweep in range(2):
                    with sp.Fori(0, CH) as c:
                        sp.wait_ge(g_free, 2 * CH * s + CH * sweep + c + 1)
                        sp.dma_start(g_adj, adj[s, c]).then_inc(g_landed, 16)
                sp.wait_ge(g_att, s + 1)
                sp.dma_start(att_dram[:, s], attg[:, :, :]).then_inc(g_stored, 16)
            sp.wait_ge(g_stored, 16 * SB + 1)

        def body(s, first, octets):
            for c in range(CH):
                n = CH * s + c
                if not (isinstance(s, int) and n < NSTAGE):
                    wait(sp, mask_ready, n - NSTAGE + 1)
                    wait(sp, byte_ready, n - NSTAGE + 1)
                    sp.dma_start(stage[:, c % NSTAGE, :], adj[s, c]).then_inc(adj_landed[c % NSTAGE], 16)
                if c == 13:
                    wait(sp, biased, s)
                    sp.dma_start(xb[:, :, :], x_in[:, s]).then_inc(x_loaded, 16)
                    with sp.If(wide_sp > 0):
                        wait(sp, att_used, s)
                        sp.dma_start(attg[:, :, :], att_dram[:, s]).then_inc(att_loaded, 16)

        superblocks(sp, body)

        for s in range(SB + 2):
            if s == 1:
                for k in range(len(BACKLOG_ROWS)):
                    sp.dma_start(backlog_sums(k), backlog_dram[:, k]).then_inc(backlog_loaded, 16)
            if s < SB:
                if s == 0:
                    sp.wait_ge(y_stored, 16 * SB)
                    sp.wait_ge(own_ready, SB)
                if s >= 2:
                    sp.wait_ge(out_stored[s % 2], 16 * (s // 2))
                sp.dma_start([xb, num][s % 2][:, :, :], y_dram[:, s]).then_inc(tail_x[s % 2], 16)
            if 1 <= s <= SB:
                sp.wait_ge(tail_out, s)
                sp.dma_start(out[:, s - 1], [xb, num][(s - 1) % 2][:, :, :]).then_inc(out_stored[(s - 1) % 2], 16)
        for k in range(2):
            sp.wait_ge(out_stored[k], 16 * SB // 2)

    @block.gpsimd
    def _(pool):
        nc.gpsimd.memset(ident[:], 0.0).then_inc(pool_consts, 1)
        nc.gpsimd.memset(one[:, :], 1.0).then_inc(backlog_stored, 1)
        pool.wait_ge(pool_consts, 1)
        nc.gpsimd.affine_select(out=ident[:], in_=ident[:], compare_op=ALU.not_equal, fill=1.0, base=0,
                                pattern=[[-1, P]], channel_multiplier=1).then_inc(pool_consts, 1)
        for b in range(BUCKETS):
            nc.gpsimd.memset(cw[:, b:b + 1], 2.0 ** -(TOP - 14 - 30 * b)).then_inc(pool_consts, 1)
        for q in range(4):
            pool.wait_ge(var_done, q + 1)
            nc.gpsimd.tensor_tensor(X[:, 16 * q:16 * q + 16, :], X[:, 16 * q:16 * q + 16, :],
                                    mv[:, 16 * q:16 * q + 16, 0].unsqueeze(2).broadcast_to([P, 16, D]),
                                    ALU.subtract).then_inc(centred, 1)
        pool.wait_ge(kmax_done, 1)
        nc.gpsimd.partition_all_reduce(ext_all, ext, P, bass.bass_isa.ReduceOp.max).then_inc(kall_done, 1)

        for q in range(4):
            pool.wait_ge(v0_hi, q + 1)
            nc.gpsimd.tensor_tensor(V0[:, 16 * q:16 * q + 16, D:2 * D], X[:, 16 * q:16 * q + 16, :],
                                    V0[:, 16 * q:16 * q + 16, 0:D], ALU.subtract).then_inc(v0_lo, 1)

        def rows(s):
            e = s - 1
            if not (isinstance(s, int) and s - 2 < FIRST_L1):
                pool.wait_ge(l1_sum, shares(s))
                nc.gpsimd.tensor_tensor(low[:, :, :], low[:, :, :], wide(dback[:, :]), ALU.mult).then_inc(l1_scaled, 1)
                pool.wait_ge(l1_scaled, shares(s))
                pool.wait_ge(own_added, s - 1)
                nc.gpsimd.tensor_tensor(yb[:, :, :], yb[:, :, :], low[:, :, :], ALU.add).then_inc(y_ready, 1)
            pool.wait_ge(z_ready, e + 1)
            if isinstance(s, int):
                pool.wait_ge(mean_cp, 1)
            nc.gpsimd.tensor_tensor(ev[:, :, 0:D], wide(zero_row[:, :]), per_block(meanh[:, :]),
                                    ALU.mult).then_inc(zrow_done, 1)
            with pool.If(wide_pool > 0):
                pool.wait_ge(att_loaded, 16 * (e + 1))
                pool.wait_ge(row_step, ROW_STEPS * (e + 1))
                nc.gpsimd.tensor_tensor(num[:, :, :], attg[:, :, :],
                                        one[:, :].unsqueeze(2).broadcast_to([P, BL, D]), ALU.mult).then_inc(att_used, 1)
                pool.wait_ge(att_used, e + 1)
            pool.wait_ge(x_loaded, 16 * (e + 1))
            pool.wait_ge(zrow_done, e + 1)
            nc.gpsimd.tensor_tensor(xb[:, :, :], xb[:, :, :], ev[:, :, 0:D], ALU.add).then_inc(xz_ready, 1)
            pool.wait_ge(h_ready, e + 1)
            wait(pool, y_stored, 16 * e)
            nc.gpsimd.tensor_tensor(yb[:, :, :], xb[:, :, :], per_block(bias[:, :]), ALU.add).then_inc(biased, 1)
            pool.wait_ge(v1_hi, e + 1)
            nc.gpsimd.tensor_tensor(V1s[:, e, :, D:2 * D], num[:, :, :], V1s[:, e, :, 0:D],
                                    ALU.subtract).then_inc(v1_ready, 1)
            nc.gpsimd.tensor_tensor(own[:, :, :], num[:, :, :], wide(dself[:, :]), ALU.mult).then_inc(own_ready, 1)
            pool.wait_ge(own_ready, e + 1)
            pool.wait_ge(biased, e + 1)
            nc.gpsimd.tensor_tensor(yb[:, :, :], yb[:, :, :], own[:, :, :], ALU.add).then_inc(own_added, 1)

        pool.wait_ge(wide_known, 1)
        wide_pool = pool.value_load(wide_f[0:1, 0:1], min_val=0, max_val=1)
        rows(1)
        rows(2)
        rows(3)
        with pool.Fori(4, SB + 1) as s:
            rows(s)

    @block.scalar
    def _(act):
        act.wait_ge(vec_consts, 2)
        for g in range(16):
            act.wait_ge(tr_done, g + 1)
            if g >= 2:
                act.wait_ge(hp_mm, g - 1)
            nc.scalar.activation(hT[g % 2], setT[g % 2][:, :], ACT.Relu).then_inc(hT_done, 1)
            if 1 <= g <= 8:
                act.wait_ge(hp_mm, g)
                copy_products(nc.scalar.copy, g - 1)
        act.wait_ge(var_done, 4)
        nc.scalar.activation(sd, mv[:, :, 1], ACT.Sqrt, bias=epsc).then_inc(std_done, 1)
        act.wait_ge(norms_done, 1)
        nc.scalar.activation(cmax, cmax, ACT.Sqrt).then_inc(norm_sqrt, 1)
        act.wait_ge(frac_done, 1)
        nc.scalar.activation(m, r1, ACT.Exp).then_inc(exp_done, 1)

        def high_parts(q):
            sl = slice(16 * q, 16 * q + 16)
            act.wait_ge(v0_f32, q + 1)
            nc.scalar.activation(V0[:, sl, 0:D], X[:, sl, :], ACT.Copy).then_inc(v0_hi, 1)

        high_parts(0)
        act.wait_ge(wide_known, 1)
        with act.If(act.value_load(wide_f[0:1, 0:1], min_val=0, max_val=1) > 0):
            with act.Fori(0, SB * T) as k:
                act.wait_ge(g_arg, k + 1)
                nc.scalar.activation(g_exp, g_exp, ACT.Exp).then_inc(g_exped, 1)

        def rows(s, part, before, stored=0):
            e = s - 1
            if part == "evac":
                act.wait_ge(l0_done, CH * (e + 1))
                wait(act, rowW_done, e)
                nc.scalar.activation(ev[:, :, :], ps0[:, :, 0:NV0], ACT.Copy).then_inc(ev_ready, 1)
            if part == "low" and not (isinstance(s, int) and s - 2 < FIRST_L1):
                act.wait_ge(l1_octet, before)
                wait(act, y_ready, shares(s) - 1)
                wait(act, backlog_stored, stored)
                nc.scalar.activation(low[:, :, :].rearrange("p (a b) f -> p a b f", b=2),
                                     ps1[:, :, :].rearrange("p a (b f) -> p a b f", b=2)[:, :, :, D:2 * D],
                                     ACT.Copy).then_inc(l1_low, 1)
            if part == "sqrt":
                act.wait_ge(sq_ready, e + 1)
                nc.scalar.activation(rs[:, :], sq[:, :], ACT.Sqrt).then_inc(sqrt_done, 1)
            if part == "relu":
                act.wait_ge(rs_ready, e + 1)
                for b in range(BL):
                    last = nc.scalar.activation(num[:, b, :], xb[:, b, :], ACT.Relu, bias=nbias[:, b:b + 1],
                                                scale=rs[:, b:b + 1])
                last.then_inc(h_ready, 1)
            if part == "store" and not (isinstance(s, int) and s < 2):
                if isinstance(s, int) and s - 2 < FIRST_L1:
                    act.wait_ge(own_added, s - 1)
                else:
                    act.wait_ge(y_ready, shares(s))
                act.dma_start(y_dram[:, s - 2], yb[:, :, :]).then_inc(y_stored, 16)
            if part == "turn":
                act.wait_ge(rowT_done, e + 1)
                nc.scalar.activation(ev[:, :, 0:D], psT[:, :].rearrange("p (b f) -> p b f", b=BL),
                                     ACT.Copy).then_inc(rowT_copied, 1)
            if part == "high":
                act.wait_ge(v_ready, e + 1)
                nc.scalar.activation(V1s[:, e, :, 0:D], num[:, :, :], ACT.Copy).then_inc(v1_hi, 1)

        def backlog(s, taken):
            act.wait_ge(l1_octet, taken)
            act.wait_ge(y_ready, shares(s))
            nc.scalar.activation(low[:, :, :], psT[:, :].rearrange("p (b f) -> p b f", b=BL),
                                 ACT.Copy).then_inc(backlog_copied, 1)
            act.wait_ge(backlog_copied, s - FIRST_BACKLOG + 1)
            act.dma_start(backlog_dram[:, s - FIRST_BACKLOG], low[:, :, :]).then_inc(backlog_stored, 16)

        def body(s, first, octets):
            stored = 0
            if octets in BACKLOG:
                stored = 16 * (s - FIRST_BACKLOG) + 1
            elif octets - 1 in BACKLOG:
                stored = 16 * len(BACKLOG_ROWS) + 1
            for c in range(CH):
                n = CH * s + c
                act.wait_ge(adj_landed[c % NSTAGE], 4 * 16 * s + 16 * (c // NSTAGE + 1))
                if c in ACT_MASKS and not (isinstance(s, int) and s == 0):
                    wait(act, l0_done, n - NMASK + 1)
                    k = CT * c + CT - 1
                    if isinstance(s, int) and s == 1 and c == ACT_MASKS[0]:
                        act.wait_ge(scale_known, 1)
                    nc.scalar.activation(mask[:, c % NMASK, (CT - 1) * IW:CT * IW],
                                         stage[:, c % NSTAGE, (CT - 1) * IW:CT * IW], ACT.Relu,
                                         scale=scale2[:, k:k + 1]).then_inc(act_mask_ready, 1)
                if c < 2:
                    if isinstance(s, int) and s == 0 and c == 0:
                        act.wait_ge(mean_mm, 1)
                        act.wait_ge(v0_f32, 1)
                    dst = bits[:, s, c * CT * IW:(c + 1) * CT * IW]
                else:
                    wait(act, packed, 14 * s + (c - 2) - 1)
                    dst = byte[:, c % 2, :]
                nc.scalar.activation(dst.rearrange("p (a l r) -> p a r l", l=P, r=2),
                                     stage[:, c % NSTAGE, :].rearrange("p (a r l) -> p a r l", l=P, r=2),
                                     ACT.Copy).then_inc(byte_ready, 1)
                if isinstance(s, int) and s == 0 and c in QUARTERS_ROUNDED:
                    high_parts(QUARTERS_ROUNDED[c])
                if not (isinstance(s, int) and s == 0):
                    for part in row_parts("act", octets, c):
                        rows(s, part, octets_before(s, first, octets), stored)
                if octets in BACKLOG and c == 13:
                    backlog(s, octets_before(s, first, octets) + len(sequence(octets)) - 1)

        superblocks(act, body)
        for part in row_order("act"):
            rows(SB, part, EARLY_OCTETS)
        act.wait_ge(own_added, SB)
        act.dma_start(y_dram[:, SB - 1], yb[:, :, :]).then_inc(y_stored, 16)

        for s in range(SB):
            act.wait_ge(l1_octet, octets_through_late(s))
            if s >= 2:
                act.wait_ge(tail_out, s - 1)
            nc.scalar.activation(tail_part(s).rearrange("p (a b) f -> p a b f", b=2),
                                 tail_ps(s).rearrange("p a (b f) -> p a b f", b=2)[:, :, :, D:2 * D],
                                 ACT.Copy).then_inc(tail_low, 1)

    @block.tensor
    def _(pe):
        pe.wait_ge(weights_in, 96)
        nc.tensor.matmul(ps1[:, 0, 0:1], waT[0:2, :], a2[0:2, :], start=True, stop=True).then_inc(w_mm, 1)
        pe.wait_ge(g_cp, 1)
        nc.tensor.matmul(ps1[:, 0, 1:2], wTt, wa2, start=True, stop=True).then_inc(w_mm, 1)
        pe.wait_ge(wsq_done, 2)
        pe.wait_ge(vec_consts, 2)
        nc.tensor.matmul(ps1[:, 1, 0:2 * D], ones, wsq, start=True, stop=True).then_inc(w_mm, 1)
        pe.wait_ge(pool_consts, 2)
        pe.wait_ge(g_cp, 2)
        for g in range(17):
            if g < 16:
                pe.wait_ge(centred, g // 4 + 1)
                if g >= 2:
                    pe.wait_ge(hT_done, g - 1)
                for b in range(4):
                    last = nc.tensor.transpose(setT[g % 2][:, b * P:(b + 1) * P], X[:, 4 * g + b, :], ident[:, :])
                last.then_inc(tr_done, 1)
            if g:
                k = g - 1
                pe.wait_ge(hT_done, k + 1)
                if k >= 2:
                    pe.wait_ge(*((hp_cp, k - 1) if k < 10 else (hp_cp2, k - 9)))
                for b in range(4):
                    last = nc.tensor.matmul(setH[k % 2][:, b // 2, (b % 2) * (D + 1):(b % 2 + 1) * (D + 1)],
                                            hT[k % 2][:, b * P:(b + 1) * P], wG, start=(b % 2 == 0), stop=(b % 2 == 1),
                                            skip_group_check=True)
                last.then_inc(hp_mm, 1)
        pe.wait_ge(rstd_done, 1)
        pe.wait_ge(hp_cp2, 8)
        for t in range(T):
            last = nc.tensor.matmul(ps1[:, 0, 128:256], rstd[:, t:t + 1].broadcast_to([P, P]), H[:, t, :],
                                    start=(t == 0), stop=(t == T - 1))
            if t in (7, T - 1):
                last.then_inc(mean_mm, 1)
        pe.wait_ge(wide_known, 1)
        with pe.If(pe.value_load(wide_f[0:1, 0:1], min_val=0, max_val=1) > 0):
            with pe.Fori(0, SB) as s:
                pe.wait_ge(g_maxed, s + 1)
                for b in range(BL):
                    last = nc.tensor.transpose(psT[:, b * P:(b + 1) * P], g_max[:, b * P:(b + 1) * P], ident[:, :])
                last.then_inc(g_turned, 1)
                pe.wait_ge(g_diag_ready, s + 1)
                nc.tensor.matmul(psH[:, :], ones, g_diag, start=True, stop=True).then_inc(g_spread, 1)

                def tile(k, begin, end):
                    pe.wait_ge(g_ready, T * s + k + 1)
                    for b in range(BL):
                        last = nc.tensor.matmul(ps0[:, b, 0:D + 1], g_prob[:, b * P:(b + 1) * P], g_h,
                                                start=begin, stop=end)
                    last.then_inc(g_mm, 1)

                tile(0, True, False)
                with pe.Fori(1, T - 1) as k:
                    tile(k, False, False)
                tile(T - 1, False, True)

        pe.wait_ge(v0_cols, 1)

        def chunk(s, c):
            n = CH * s + c
            pe.wait_ge(mask_ready, n + 1)
            for t in range(CT):
                k = CT * c + t
                if c in ACT_MASKS and t == CT - 1 and not (isinstance(s, int) and s == 0):
                    pe.wait_ge(act_mask_ready, act_masks_through(s, c))
                for b in range(BL):
                    last = nc.tensor.matmul(ps0[:, b, 0:NV0], mask[:, c % NMASK, t * IW + b * P:t * IW + (b + 1) * P],
                                            V0[:, k, :], start=(k == 0), stop=(k == T - 1))
            last.then_inc(l0_done, 1)

        def octet(sums, count, o, slot, begin, end):
            pe.wait_ge(unpacked, count + 1)
            for t in range(OCT):
                for b in range(BL):
                    last = nc.tensor.matmul(sums[:, b // 2, (b % 2) * 2 * D:(b % 2 + 1) * 2 * D],
                                            unp[:, slot, b % 2, t * 256 + (b // 2) * P:t * 256 + (b // 2 + 1) * P],
                                            V1[:, OCT * o + t, :], start=(begin and t == 0 and b % 2 == 0),
                                            stop=(end and t == OCT - 1), skip_group_check=True)
            return last

        def backlog_octet(count, o, slot, begin, end):
            pe.wait_ge(unpacked, count + 1)
            for t in range(OCT):
                for b in range(BL):
                    for part in range(2):
                        last = nc.tensor.matmul(psT[:, b * P:(b + 1) * P],
                                                unp[:, slot, b % 2, t * 256 + (b // 2) * P:t * 256 + (b // 2 + 1) * P],
                                                V1[:, OCT * o + t, part * D:(part + 1) * D],
                                                start=(begin and t == 0 and b == 0 and part == 0),
                                                stop=(end and t == OCT - 1), skip_group_check=True)
            return last

        def rows(s, part):
            e = s - 1
            if part == "turn":
                pe.wait_ge(h_ready, e + 1)
                for b in range(BL):
                    last = nc.tensor.transpose(psT[:, b * P:(b + 1) * P], num[:, b, :], ident[:, :])
                last.then_inc(rowT_done, 1)
            if part == "weigh":
                pe.wait_ge(rowT_copied, e + 1)
                wait(pe, v_ready, e)
                for b in range(BL):
                    last = nc.tensor.matmul(psH[:, b * P:(b + 1) * P], ev[:, b, 0:D], WT[:, :],
                                            start=(b == 0), stop=(b == BL - 1), skip_group_check=True)
                last.then_inc(rowW_done, 1)

        def body(s, first, octets):
            for c in range(CH):
                if c == 0:
                    take(s, first, octets, -1)
                    if isinstance(s, int) and s == 0:
                        pe.wait_ge(v0_lo, 1)
                    else:
                        pe.wait_ge(ev_ready, s)
                if isinstance(s, int) and s == 0 and c % 4 == 0 and c:
                    pe.wait_ge(v0_lo, c // 4 + 1)
                chunk(s, c)
                if not (isinstance(s, int) and s == 0):
                    for part in row_parts("pe", octets, c):
                        rows(s, part)
                take(s, first, octets, c)

        def take(s, first, octets, c):
            before = octets_before(s, first, octets)
            for q, (at, back, o) in enumerate(sequence(octets)):
                if at != c:
                    continue
                pe.wait_ge(v1_ready, 2 * o + 2)
                if back:
                    last = backlog_octet(before + q, o, q % 2, o == BACKLOG[octets][1][0][1],
                                         o == BACKLOG[octets][1][-1][1])
                    last.then_inc(l1_octet, 1)
                    continue
                if isinstance(s, int) and s - 2 < FIRST_L1:
                    pe.wait_ge(mean_cp, 1)
                elif o == 0:
                    pe.wait_ge(l1_sum, shares(s))
                octet(ps1, before + q, o, q % 2, o == 0, o == octets - 1).then_inc(l1_octet, 1)

        superblocks(pe, body)

        for count, (s, o) in enumerate(LATE_OCTETS, EARLY_OCTETS):
            if o == LATE_OF[s][0]:
                wait(pe, tail_sum, s - 1)
                if s == 0:
                    pe.wait_ge(ev_ready, SB)
            if (s, o) == LATE_OCTETS[LAST_OF[0]]:
                pe.wait_ge(v1_ready, SB)
            octet(tail_ps(s), count, o, count % 2, o == LATE_OF[s][0], o == LATE_OF[s][-1]).then_inc(l1_octet, 1)
            for part in {3: ["turn"], 5: ["weigh"]}.get(count - EARLY_OCTETS, ()):
                rows(SB, part)

    def own_maxima(dve):
        steps = 3 * T + 6
        f_of = f.rearrange("p (c t) -> p c t", t=CT)
        fs_of = fs.rearrange("p (c t) -> p c t", t=CT)
        rstd_of = rstd.rearrange("p (c t) -> p c t", t=CT)
        H_of = H.rearrange("p (c t) f -> p c t f", t=CT)

        def step(ins, n):
            ins.then_inc(g_vec, 1)
            dve.wait_ge(g_vec, n)

        step(nc.vector.tensor_scalar(nf1, ext_all[:, 1:2], 1.0, None, ALU.add), 1)
        nc.vector.tensor_scalar(fs, f, nf1, 0.5, ALU.add, ALU.max).then_inc(g_vec, 1)
        nc.vector.memset(g_max, 0.0).then_inc(g_vec, 1)
        nc.vector.memset(g_h[:, D:D + 1], 1.0).then_inc(g_free, 1)
        nc.vector.memset(g_den, 0.0).then_inc(g_mm, 1)
        nc.vector.memset(g_col, 0.0).then_inc(g_stored, 1)
        with dve.Fori(0, SB) as s:
            at = steps * s + 3

            with dve.Fori(0, CH) as c:
                dve.wait_ge(g_landed, 16 * (2 * CH * s + c) + 16)
                dve.wait_ge(g_free, 2 * CH * s + c + 1)
                for t in range(CT):
                    n = at + 2 * CT * c + 2 * t
                    dve.wait_ge(g_vec, n)
                    step(nc.vector.tensor_scalar(g_tmp, g_adj[:, t * IW:(t + 1) * IW], 0.0, fs_of[:, c, t:t + 1],
                                                 ALU.is_gt, ALU.mult), n + 1)
                    step(nc.vector.tensor_tensor(g_max, g_max, g_tmp, ALU.max), n + 2)
                nc.vector.memset(g_zero, 0.0).then_inc(g_free, 1)
            nc.vector.memset(g_den, 0.0).then_inc(g_maxed, 1)
            at = at + 2 * T
            dve.wait_ge(g_turned, s + 1)
            step(nc.vector.tensor_reduce(g_col, psT[:, :].rearrange("p (b f) -> p b f", b=BL), AX.X, ALU.max), at + 1)
            nc.vector.tensor_tensor(g_diag.rearrange("p (b f) -> p b f", b=BL), per_block(ident[:, :]), wide(g_col),
                                    ALU.mult).then_inc(g_diag_ready, 1)
            dve.wait_ge(g_spread, s + 1)
            nc.vector.tensor_scalar(g_shift, psH[:, :], -1.0, nf1, ALU.mult, ALU.add).then_inc(g_vec, 1)
            at = at + 2

            with dve.Fori(0, CH) as c:
                dve.wait_ge(g_landed, 16 * (2 * CH * s + CH + c) + 16)
                dve.wait_ge(g_free, 2 * CH * s + CH + c + 1)
                for t in range(CT):
                    k = CT * c + t
                    dve.wait_ge(g_vec, at + k)
                    nc.vector.tensor_scalar(g_exp, g_shift, f_of[:, c, t:t + 1], 20.0, ALU.add,
                                            ALU.min).then_inc(g_arg, 1)
                    dve.wait_ge(g_mm, T * s + k + 1)
                    nc.vector.tensor_scalar(g_h[:, 0:D], H_of[:, c, t, :], rstd_of[:, c, t:t + 1], None,
                                            ALU.mult).then_inc(g_vec, 1)
                    dve.wait_ge(g_exped, T * s + k + 1)
                    dve.wait_ge(g_vec, at + k + 1)
                    nc.vector.scalar_tensor_tensor(g_prob, g_adj[:, t * IW:(t + 1) * IW], 0.0, g_exp, ALU.is_gt,
                                                   ALU.mult).then_inc(g_ready, 1)
                    dve.wait_ge(g_ready, T * s + k + 1)
                nc.vector.memset(g_zero, 0.0).then_inc(g_free, 1)
            at = at + T
            dve.wait_ge(g_mm, T * s + T + 1)
            dve.wait_ge(g_free, 2 * CH * (s + 1) + 1)
            step(nc.vector.tensor_scalar(g_zero, ps0[:, :, D], 0.0, None, ALU.is_equal), at + 1)
            step(nc.vector.tensor_tensor(g_den, g_zero, ps0[:, :, D], ALU.add), at + 2)
            step(nc.vector.reciprocal(g_den, g_den), at + 3)
            dve.wait_ge(g_stored, 16 * s + 1)
            nc.vector.tensor_tensor(attg[:, :, :], ps0[:, :, 0:D], wide(g_den), ALU.mult).then_inc(g_att, 1)
            dve.wait_ge(g_att, s + 1)
            nc.vector.memset(g_max, 0.0).then_inc(g_vec, 1)

    @block.vector
    def _(dve):
        steps = [0]

        def link(ins):
            steps[0] += 1
            ins.then_inc(vec_step, 1)
            dve.wait_ge(vec_step, steps[0])

        nc.vector.memset(ones, 1.0).then_inc(vec_consts, 1)
        nc.vector.memset(epsc, EPS).then_inc(vec_consts, 1)

        def stats(q):
            dve.wait_ge(x_part[q], 16)
            for t in range(16 * q, 16 * q + 16):
                last = nc.vector.bn_stats(st[:, t, :], X[:, t, :])
            link(last)
            for t in range(16 * q, 16 * q + 16):
                last = nc.vector.bn_aggr(mv[:, t, :], st[:, t, :])
            last.then_inc(var_done, 1)

        stats(0)
        dve.wait_ge(weights_in, 96)
        nc.vector.tensor_tensor(wsq[:, 0:D], wG[:, 0:D], wG[:, 0:D], ALU.mult).then_inc(wsq_done, 1)
        nc.vector.tensor_tensor(wsq[:, D:2 * D], WT[:, :], WT[:, :], ALU.mult).then_inc(wsq_done, 1)
        dve.wait_ge(w_mm, 1)
        nc.vector.tensor_copy(wa2, ps1[:, 0, 0:1]).then_inc(g_cp, 1)
        dve.wait_ge(w_mm, 2)
        nc.vector.tensor_copy(wG[:, D:D + 1], ps1[:, 0, 1:2]).then_inc(g_cp, 1)
        stats(1)
        dve.wait_ge(w_mm, 3)
        for k in range(2):
            link(nc.vector.tensor_reduce(cmax[:, k:k + 1], ps1[:, 1, k * D:(k + 1) * D], AX.X, ALU.max))
        nc.vector.tensor_scalar(cmax, cmax, 1e-30, None, ALU.max).then_inc(norms_done, 1)
        stats(2)
        stats(3)
        for g in range(8, 16):
            dve.wait_ge(hp_mm, g + 1)
            copy_products(nc.vector.tensor_copy, g)
        dve.wait_ge(std_done, 1)
        nc.vector.reciprocal(rstd, sd).then_inc(rstd_done, 1)
        dve.wait_ge(norm_sqrt, 1)
        link(nc.vector.reciprocal(sig[:, 6:8], cmax))
        link(nc.vector.tensor_scalar(sig[:, 6:8], sig[:, 6:8], BOUND, None, ALU.mult))
        link(nc.vector.tensor_scalar(sig[:, 0:2].bitcast(U32), sig[:, 6:8].bitcast(U32), 0x7F800000, None,
                                     ALU.bitwise_and))
        link(nc.vector.tensor_scalar(sig[:, 2:3], sig[:, 0:1], 1.0 / M_SCALE, None, ALU.mult))
        link(nc.vector.reciprocal(sig[:, 3:4], sig[:, 1:2]))
        link(nc.vector.tensor_scalar(sig[:, 4:5], sig[:, 3:4], 0.5, None, ALU.mult))
        dve.wait_ge(rstd_done, 1)
        dve.wait_ge(hp_cp, 8)
        dve.wait_ge(hp_cp2, 8)
        link(nc.vector.tensor_tensor(f, f, rstd, ALU.mult))
        link(nc.vector.tensor_scalar(kf, f, LOG2E, ROUND, ALU.mult, ALU.add))
        link(nc.vector.tensor_scalar(kf, kf, -ROUND, None, ALU.add))
        link(nc.vector.tensor_reduce(ext[:, 1:2], f, AX.X, ALU.min))
        link(nc.vector.tensor_scalar(ext[:, 1:2], ext[:, 1:2], -1.0, None, ALU.mult))
        nc.vector.tensor_reduce(ext[:, 0:1], kf, AX.X, ALU.max).then_inc(kmax_done, 1)
        link(nc.vector.scalar_tensor_tensor(r1, kf, -LN2_HI, f, ALU.mult, ALU.add))
        nc.vector.scalar_tensor_tensor(r1, kf, -LN2_LO, r1, ALU.mult, ALU.add).then_inc(frac_done, 1)
        dve.wait_ge(exp_done, 1)
        link(nc.vector.scalar_tensor_tensor(mS, m, sig[:, 0:1], rstd, ALU.mult, ALU.mult))

        def scaled_products(q):
            sl = slice(16 * q, 16 * q + 16)
            nc.vector.tensor_tensor(X[:, sl, :], H[:, sl, :], wide(mS[:, sl]), ALU.mult).then_inc(v0_f32, 1)

        scaled_products(0)
        link(nc.vector.tensor_scalar(m, m, M_SCALE, None, ALU.mult))
        link(nc.vector.tensor_copy(V0[:, :, 2 * D], m))
        nc.vector.tensor_tensor(V0[:, :, 2 * D + 1], m, V0[:, :, 2 * D], ALU.subtract)
        dve.wait_ge(kall_done, 1)
        link(nc.vector.scalar_tensor_tensor(spread, kall, math.log(2.0), ext_all[:, 1:2], ALU.mult, ALU.add))
        nc.vector.tensor_scalar(wide_f[:, :], spread, SPREAD, None, ALU.is_gt).then_inc(wide_known, 1)
        link(nc.vector.tensor_scalar(ke, kf, kall, float(TOP), ALU.subtract, ALU.add))
        link(nc.vector.tensor_scalar(ke, ke, float(LOW), None, ALU.max))
        link(nc.vector.tensor_scalar(sbit, ke, 127.0, float(2 ** 23), ALU.add, ALU.mult))
        nc.vector.tensor_copy(scale2[:, :].bitcast(I32), sbit).then_inc(scale_known, 1)
        dve.wait_ge(scale_known, 1)
        def count_columns():
            for b in range(BUCKETS):
                last = nc.vector.tensor_scalar(w15[b], ke, -1.0, float(TOP - 14 - 30 * b + 15), ALU.mult, ALU.add)
            link(last)
            for b in range(BUCKETS):
                last = nc.vector.scalar_tensor_tensor(q1[b], w15[b], 1.0, w15[b], ALU.is_ge, ALU.mult)
            link(last)
            for b in range(BUCKETS):
                last = nc.vector.scalar_tensor_tensor(q2[b], w15[b], 30.0, q1[b], ALU.is_le, ALU.mult)
            link(last)
            for b in range(BUCKETS):
                last = nc.vector.tensor_scalar(V0[:, :, 2 * D + 2 + b].bitcast(U16), q2[b], 1024.0, None, ALU.mult)
            last.then_inc(v0_cols, 1)

        dve.wait_ge(wide_known, 1)
        with dve.If(dve.value_load(wide_f[0:1, 0:1], min_val=0, max_val=1) > 0):
            own_maxima(dve)

        def pack(s, c):
            if c < 2:
                return
            dve.wait_ge(byte_ready, CH * s + c + 1)
            if c >= 4:
                dve.wait_ge(packed, 14 * s + (c - 2) - 1)
            dst = bits[:, s, (c % 2) * CT * IW:(c % 2 + 1) * CT * IW].bitcast(U32)
            nc.vector.scalar_tensor_tensor(dst, byte[:, c % 2, :].bitcast(U32), c // 2, dst,
                                           ALU.logical_shift_left, ALU.bitwise_or).then_inc(packed, 1)

        def unpack(s, o, slot, free):
            wait(dve, l1_octet, free)
            for par in range(2):
                shift = 14 - o - 8 * par
                last = nc.vector.tensor_scalar(
                    unp[:, slot, par, :].bitcast(U32), bits[:, s, :].bitcast(U32), abs(shift), 0x40004000,
                    ALU.logical_shift_left if shift >= 0 else ALU.logical_shift_right, ALU.bitwise_and)
            last.then_inc(unpacked, 1)

        def rows(s, part):
            e = s - 1

            def step(ins, k):
                ins.then_inc(row_step, 1)
                dve.wait_ge(row_step, ROW_STEPS * e + k)

            if part == "sums":
                dve.wait_ge(ev_ready, e + 1)
                wait(dve, own_ready, e)
                nc.vector.tensor_tensor(cprod[:, :, :], ev[:, :, 2 * D + 2:NV0],
                                        cw[:, :].unsqueeze(1).broadcast_to([P, BL, BUCKETS]), ALU.mult)
                step(nc.vector.tensor_tensor(den[:, :], ev[:, :, 2 * D], ev[:, :, 2 * D + 1], ALU.add), 1)
                step(nc.vector.tensor_reduce(cnt[:, :], cprod[:, :, :], AX.X, ALU.add), 2)
                nc.vector.tensor_tensor(num[:, :, :], ev[:, :, 0:D], ev[:, :, D:2 * D], ALU.add)
                step(nc.vector.tensor_scalar(zero_row[:, :], cnt[:, :], 0.0, None, ALU.is_equal), 3)
                nc.vector.scalar_tensor_tensor(den[:, :], den[:, :], sig[:, 2:3], zero_row[:, :], ALU.mult,
                                               ALU.add).then_inc(z_ready, 1)
                dve.wait_ge(z_ready, e + 1)
                step(nc.vector.reciprocal(rden[:, :], den[:, :]), 4)
                step(nc.vector.tensor_tensor(num[:, :, :], num[:, :, :], wide(rden[:, :]), ALU.mult), 5)
            if part == "stats":
                dve.wait_ge(xz_ready, e + 1)
                nc.vector.scalar_tensor_tensor(xb[:, :, :], num[:, :, :], 0.0, xb[:, :, :], ALU.max,
                                               ALU.add).then_inc(x1_ready, 1)
                dve.wait_ge(x1_ready, e + 1)
                for b in range(BL):
                    last = nc.vector.bn_stats(bst[:, b, :], xb[:, b, :])
                last.then_inc(rstat_done, 1)
                dve.wait_ge(rstat_done, 2 * e + 1)
                nc.vector.tensor_scalar(sq[:, BL:2 * BL], cnt[:, :], 1.0, None, ALU.add)
                for b in range(BL):
                    last = nc.vector.bn_aggr(bmv[:, b, :], bst[:, b, :])
                last.then_inc(rstat_done, 1)
                dve.wait_ge(rstat_done, 2 * e + 2)
                nc.vector.tensor_scalar(sq[:, 0:BL], bmv[:, :, 1], EPS, None, ALU.add).then_inc(sq_ready, 1)
            if part == "scales":
                if not (isinstance(s, int) and s - 2 < FIRST_L1):
                    dve.wait_ge(y_ready, shares(s))
                dve.wait_ge(sqrt_done, e + 1)
                nc.vector.reciprocal(rs[:, :], rs[:, :]).then_inc(rs_recip, 1)
                dve.wait_ge(rs_recip, e + 1)
                nc.vector.scalar_tensor_tensor(nbias[:, :], bmv[:, :, 0], -1.0, rs[:, 0:BL], ALU.mult, ALU.mult)
                nc.vector.tensor_copy(dalls[:, e, :], rs[:, BL:2 * BL])
                nc.vector.tensor_scalar(dsig[:, :], rs[:, BL:2 * BL], sig[:, 1:2], None, ALU.mult)
                nc.vector.tensor_scalar(dself[:, :], rs[:, BL:2 * BL], sig[:, 3:4], None, ALU.mult)
                nc.vector.tensor_scalar(dback[:, :], rs[:, BL:2 * BL], sig[:, 4:5], None,
                                        ALU.mult).then_inc(rs_ready, 1)
            if part == "low" and not (isinstance(s, int) and s - 2 < FIRST_L1):
                dve.wait_ge(l1_low, shares(s))
                part4 = low[:, :, :].rearrange("p (a b) f -> p a b f", b=2)
                nc.vector.tensor_tensor(part4, ps1[:, :, :].rearrange("p a (b f) -> p a b f", b=2)[:, :, :, 0:D],
                                        part4, ALU.add).then_inc(l1_sum, 1)
            if part == "v":
                dve.wait_ge(rowW_done, e + 1)
                dve.wait_ge(rs_ready, e + 1)
                nc.vector.tensor_tensor(num[:, :, :], psH[:, :].rearrange("p (b f) -> p b f", b=BL),
                                        wide(dsig[:, :]), ALU.mult).then_inc(v_ready, 1)

        def body(s, first, octets):
            place = {at: q for q, (at, _, _) in enumerate(sequence(octets))}

            def take(c):
                if c in place:
                    q = place[c]
                    _, back, o = sequence(octets)[q]
                    if q == 0:
                        dve.wait_ge(packed, 14 * s)
                    unpack(s - (back or 1), o, q % 2, octets_before(s, first, octets) + max(q - 1, 0))

            take(-1)
            for c in range(CH):
                n = CH * s + c
                dve.wait_ge(adj_landed[c % NSTAGE], 4 * 16 * s + 16 * (c // NSTAGE + 1))
                wait(dve, l0_done, n - NMASK + 1)
                for t in range(CT - (c in ACT_MASKS and not (isinstance(s, int) and s == 0))):
                    k = CT * c + t
                    last = nc.vector.tensor_scalar(mask[:, c % NMASK, t * IW:(t + 1) * IW],
                                                   stage[:, c % NSTAGE, t * IW:(t + 1) * IW], 0.0,
                                                   scale2[:, k:k + 1], ALU.is_gt, ALU.mult)
                last.then_inc(mask_ready, 1)
                if isinstance(s, int) and s == 0:
                    if c == 2:
                        count_columns()
                    if c in QUARTERS_SCALED:
                        scaled_products(QUARTERS_SCALED[c])
                    if c == 3:
                        dve.wait_ge(mean_mm, 2)
                        nc.vector.tensor_scalar(meanh[:, :], ps1[:, 0, 128:256], 1.0 / N, 0.0, ALU.mult,
                                                ALU.max).then_inc(mean_cp, 1)
                pack(s, c)
                if not (isinstance(s, int) and s == 0):
                    for part in row_parts("dve", octets, c):
                        rows(s, part)
                take(c)

        superblocks(dve, body)

        def finish(s):
            ybuf = [xb, num][s % 2]
            part = tail_part(s)
            part4 = part.rearrange("p (a b) f -> p a b f", b=2)
            dve.wait_ge(tail_low, s + 1)
            nc.vector.tensor_tensor(part4, tail_ps(s).rearrange("p a (b f) -> p a b f", b=2)[:, :, :, 0:D], part4,
                                    ALU.add).then_inc(tail_sum, 1)
            dve.wait_ge(tail_sum, s + 1)
            for k, row in enumerate(BACKLOG_ROWS):
                if row == s:
                    if k == 0:
                        dve.wait_ge(backlog_loaded, 16 * len(BACKLOG_ROWS))
                    nc.vector.tensor_tensor(part, part, backlog_sums(k), ALU.add).then_inc(backlog_added, 1)
                    dve.wait_ge(backlog_added, k + 1)
            dve.wait_ge(dall_done, 1)
            nc.vector.tensor_tensor(part, part, wide(dalls[:, s, :]), ALU.mult).then_inc(tail_scaled, 1)
            dve.wait_ge(tail_scaled, s + 1)
            dve.wait_ge(tail_x[s % 2], 16 * (s // 2 + 1))
            nc.vector.tensor_tensor(ybuf[:, :, :], ybuf[:, :, :], part, ALU.add).then_inc(tail_out, 1)

        dve.wait_ge(packed, 14 * SB)
        for count, (s, o) in enumerate(LATE_OCTETS, EARLY_OCTETS):
            unpack(s, o, count % 2, max(EARLY_OCTETS, count - 1))
            k = count - EARLY_OCTETS
            for part in {1: ["low", "sums"], 2: ["stats"], 3: ["scales"], 6: ["v"]}.get(k, ()):
                rows(SB, part)
            if k - 2 in LAST_OF:
                before = LAST_OF.index(k - 2)
                if before == 0:
                    nc.vector.tensor_scalar(dall[:, :], dall[:, :], sig[:, 4:5], None, ALU.mult).then_inc(dall_done, 1)
                finish(before)
        finish(SB - 1)

    ctx.close()


_INS = [("adj", (SB, CH, P, CT * IW)), ("x", (P, SB, BL, D)), ("w", (D, D)), ("wT", (D, D)), ("waT", (2, D)),
        ("a", (2, 1)), ("WT", (D, D)), ("b", (P, D))]


def kernel(x, adj, L0_gnn_w, L0_gnn_w_a, L0_gnn_a, L1_gnn_W, L1_gnn_b):
    import concourse.bacc as bacc
    from concourse.bass_utils import run_bass_kernel_spmd

    x, adj, w, w_a, a, W, b = (np.asarray(v) for v in (x, adj, L0_gnn_w, L0_gnn_w_a, L0_gnn_a, L1_gnn_W, L1_gnn_b))
    chunks = adj.reshape(SB, IW, CH, CT, P).transpose(0, 2, 4, 3, 1).reshape(SB, CH, P, CT * IW)
    arrays = {
        "adj": np.ascontiguousarray(chunks),
        "x": np.ascontiguousarray(x.reshape(T, P, D).transpose(1, 0, 2)).reshape(P, SB, BL, D),
        "w": np.ascontiguousarray(w),
        "wT": np.ascontiguousarray(w.T),
        "waT": np.ascontiguousarray(w_a.T),
        "a": np.ascontiguousarray(a[2:4]),
        "WT": np.ascontiguousarray(W.T),
        "b": np.ascontiguousarray(np.broadcast_to(b[None, :], (P, D))),
    }
    nc = bacc.Bacc("TRN2", target_bir_lowering=False, num_devices=1, dynamic_dma_scratch_size=1024)
    ins = [nc.dram_tensor(f"{name}_in", shape, F32, kind="ExternalInput").ap() for name, shape in _INS]
    out = nc.dram_tensor("out", (P, SB, BL, D), F32, kind="ExternalOutput").ap()
    build(nc, ins, out)
    r = run_bass_kernel_spmd(nc, [{f"{k}_in": v for k, v in arrays.items()}], core_ids=[0])
    got = r.results[0]["out"]
    return np.ascontiguousarray(got.reshape(P, T, D).transpose(1, 0, 2)).reshape(N, D)
```
